# Optimizing a Trainium2 kernel written in Bass

```python
import numpy as np
import jax
import jax.numpy as jnp

def _softmax(x, axis=-1):
    return jax.nn.softmax(x, axis=axis)

def _gelu(x):
    return jax.nn.gelu(x, approximate=True)

def _silu(x):
    return jax.nn.silu(x)

def _sigmoid(x):
    return jax.nn.sigmoid(x)

def _layernorm(x, axis=-1, eps=1e-05):
    m = jnp.mean(x, axis=axis, keepdims=True)
    v = jnp.var(x, axis=axis, keepdims=True)
    return (x - m) / jnp.sqrt(v + eps)

def _scatter_add(tgt, idx, src, axis=0):
    return tgt.at[idx].add(src)

def _segment_sum(src, seg, n):
    return jax.ops.segment_sum(src, seg, n)
kernel_name = 'mk_gnn_preln_d2_gnn_r8_1e467a'

def setup_inputs(seed: int=0):
    np.random.seed(seed)
    _w = jnp.asarray

    def _rec_inputs():
        import jax
        import jax.numpy as jnp
        _gk = jax.random.key(seed)
        x = -0.0003713 + 1 * jax.random.normal(jax.random.fold_in(_gk, 1), (6250, 256), jnp.float32)
        _s = jax.random.randint(jax.random.fold_in(_gk, 2), (100000,), 0, 6250, jnp.int32)
        _d = jax.random.randint(jax.random.fold_in(_gk, 3), (100000,), 0, 6250, jnp.int32)
        _loop = jnp.arange(6250, dtype=jnp.int32)
        src = jnp.concatenate([_s, _d, _loop])
        dst = jnp.concatenate([_d, _s, _loop])
        _o = jnp.argsort(dst, stable=True)
        src = src[_o]
        dst = dst[_o]
        edge_attr_2 = jax.random.uniform(jax.random.fold_in(_gk, 12), (206250, 2), jnp.float32, 0.0, 1)
        edge_attr_64 = -9.77346e-05 + 0.999888 * jax.random.normal(jax.random.fold_in(_gk, 13), (206250, 64), jnp.float32)
        return (x, src, dst, edge_attr_2, edge_attr_64)
    x, src, dst, edge_attr_2, edge_attr_64 = _rec_inputs()

    def _L0_gnn_setup():
        import jax, jax.numpy as jnp
        import numpy as np
        N, E = (6250, 100000)
        IN_FEATS, EDGE_FEATS = (256, 64)
        H, F = (8, 32)
        LRELU_SLOPE = 0.01
        key = jax.random.key(seed)
        ks = jax.random.split(key, 9)
        return {'h': jax.random.normal(ks[0], (N, IN_FEATS), jnp.float32), 'edge_features': jax.random.normal(ks[1], (E, EDGE_FEATS), jnp.float32), 'src': jax.random.randint(ks[2], (E,), 0, N, jnp.int32), 'dst': jax.random.randint(ks[3], (E,), 0, N, jnp.int32), 'W_w': jax.random.normal(ks[4], (IN_FEATS, H * F), jnp.float32) * 0.05, 'We_w': jax.random.normal(ks[5], (EDGE_FEATS, H * F), jnp.float32) * 0.05, 'a_src': jax.random.normal(ks[6], (H, F), jnp.float32) * 0.1, 'a_dst': jax.random.normal(ks[7], (H, F), jnp.float32) * 0.1, 'a_edge': jax.random.normal(ks[8], (H, F), jnp.float32) * 0.1}
    _L0_gnn_all = _L0_gnn_setup()
    _L0_gnn_in = {k: v for k, v in _L0_gnn_all.items() if k in ('W_w', 'We_w', 'a_src', 'a_dst', 'a_edge')}
    del _L0_gnn_all

    def _L1_gnn_setup():
        import jax, jax.numpy as jnp
        import numpy as np
        N_NODES = 12500
        N_EDGES = 200000
        IN_FEATS = 256
        OUT_FEATS = 64
        NUM_HEADS = 4
        key = jax.random.key(seed)
        k_h, k_adj, k_dir, k_wf, k_wr, k_af = jax.random.split(key, 6)
        h = jax.random.normal(k_h, (N_NODES, IN_FEATS), dtype=jnp.float32)
        adj = jax.random.randint(k_adj, (2, N_EDGES), 0, N_NODES, dtype=jnp.int64)
        bit = jax.random.randint(k_dir, (N_EDGES,), 0, 2).astype(jnp.float32)
        direction = jnp.stack([bit, 1.0 - bit], axis=1)
        s_w = float(np.sqrt(6.0 / (IN_FEATS + OUT_FEATS)))
        s_a = float(np.sqrt(6.0 / (NUM_HEADS + OUT_FEATS)))
        W_forward = jax.random.uniform(k_wf, (OUT_FEATS, IN_FEATS), jnp.float32, -s_w, s_w)
        W_reverse = jax.random.uniform(k_wr, (OUT_FEATS, IN_FEATS), jnp.float32, -s_w, s_w)
        attn_forward = jax.random.uniform(k_af, (1, NUM_HEADS, OUT_FEATS), jnp.float32, -s_a, s_a)
        return {'h': h, 'adj': adj, 'direction': direction, 'W_forward': W_forward, 'W_reverse': W_reverse, 'attn_forward': attn_forward}
    _L1_gnn_all = _L1_gnn_setup()
    _L1_gnn_in = {k: v for k, v in _L1_gnn_all.items() if k in ('W_forward', 'W_reverse', 'attn_forward')}
    del _L1_gnn_all
    return {'x': x, 'src': src, 'dst': dst, 'edge_attr_2': edge_attr_2, 'edge_attr_64': edge_attr_64, 'L0_gnn_W_w': _L0_gnn_in['W_w'], 'L0_gnn_We_w': _L0_gnn_in['We_w'], 'L0_gnn_a_src': _L0_gnn_in['a_src'], 'L0_gnn_a_dst': _L0_gnn_in['a_dst'], 'L0_gnn_a_edge': _L0_gnn_in['a_edge'], 'L1_gnn_W_forward': _L1_gnn_in['W_forward'], 'L1_gnn_W_reverse': _L1_gnn_in['W_reverse'], 'L1_gnn_attn_forward': _L1_gnn_in['attn_forward']}

def reference(x, src, dst, edge_attr_2, edge_attr_64, L0_gnn_W_w, L0_gnn_We_w, L0_gnn_a_src, L0_gnn_a_dst, L0_gnn_a_edge, L1_gnn_W_forward, L1_gnn_W_reverse, L1_gnn_attn_forward):
    import jax
    import jax.numpy as jnp

    def _L0_gnn_ref(h, edge_features, src, dst, W_w, We_w, a_src, a_dst, a_edge):
        import jax, jax.numpy as jnp
        import numpy as np
        N, E = (6250, 100000)
        IN_FEATS, EDGE_FEATS = (256, 64)
        H, F = (8, 32)
        LRELU_SLOPE = 0.01
        Wh = (h @ W_w).reshape(-1, H, F)
        We = (edge_features @ We_w).reshape(-1, H, F)
        s = jnp.einsum('ehf,hf->eh', Wh[src], a_src) + jnp.einsum('ehf,hf->eh', Wh[dst], a_dst) + jnp.einsum('ehf,hf->eh', We, a_edge)
        s = jnp.where(s > 0, s, LRELU_SLOPE * s)
        m = jax.ops.segment_max(s, dst, num_segments=N)
        ex = jnp.exp(s - m[dst])
        den = jax.ops.segment_sum(ex, dst, num_segments=N)
        a = ex / den[dst]
        msg = Wh[src] * a[:, :, None]
        h_new = jax.ops.segment_sum(msg, dst, num_segments=N)
        h_new = h_new.reshape(-1, H * F)
        return jax.nn.elu(h_new)

    def _L1_gnn_ref(h, adj, direction, W_forward, W_reverse, attn_forward):
        import jax, jax.numpy as jnp
        import numpy as np
        N_NODES = 12500
        N_EDGES = 200000
        IN_FEATS = 256
        OUT_FEATS = 64
        NUM_HEADS = 4
        N = h.shape[0]
        H = attn_forward.shape[1]
        h_fwd = h @ W_forward.T
        h_rev = h @ W_reverse.T
        src, dst = (adj[0], adj[1])
        messages = h_fwd[src] * direction[:, 0:1] + h_rev[src] * direction[:, 1:2]
        scores = jnp.einsum('ef,hf->eh', messages, attn_forward[0])
        scores = jax.nn.leaky_relu(scores, negative_slope=0.2)
        exp_scores = jnp.exp(scores - scores.max(axis=0, keepdims=True))
        sum_exp = jax.ops.segment_sum(exp_scores, dst, num_segments=N)
        norm = exp_scores / (sum_exp[dst] + 1e-10)
        outs = [jax.ops.segment_sum(messages * norm[:, hd:hd + 1], dst, num_segments=N) for hd in range(H)]
        out = jnp.stack(outs, axis=1)
        return out.reshape(N, -1)
    edge_index = jnp.stack([src, dst])
    h = jnp.maximum(_layernorm(x, axis=-1), 0.0)
    x = x + _L0_gnn_ref(h, edge_attr_64, src, dst, L0_gnn_W_w, L0_gnn_We_w, L0_gnn_a_src, L0_gnn_a_dst, L0_gnn_a_edge)
    h = jnp.maximum(_layernorm(x, axis=-1), 0.0)
    x = x + _L1_gnn_ref(h, edge_index, edge_attr_2, L1_gnn_W_forward, L1_gnn_W_reverse, L1_gnn_attn_forward)
    return x

_drawn_inputs = setup_inputs


def setup_inputs(seed=0):
    import zlib

    import numpy as np

    out = dict(_drawn_inputs(seed))
    spreads = {}
    factors = {'edge_attr_64': 4.866,
     'L0_gnn_We_w': 4.839,
     'L0_gnn_a_src': 2.708,
     'L0_gnn_a_dst': 55.64,
     'L0_gnn_a_edge': 4.706}
    for name, (base, spread) in spreads.items():
        noise = np.random.default_rng([zlib.crc32(name.encode()), seed]).standard_normal(out[name].shape)
        drawn = base * np.exp(spread * noise) if base else spread * noise
        out[name] = jnp.asarray(drawn.astype(out[name].dtype))
    for name, factor in factors.items():
        out[name] = (out[name] * factor).astype(out[name].dtype)
    return out
```

```python
from contextlib import ExitStack

import concourse.bass as bass
from concourse import mybir

F32 = mybir.dt.float32
I32 = mybir.dt.int32
ALU = mybir.AluOpType
ACT = mybir.ActivationFunctionType
AX_X = mybir.AxisListType.X

P = 128
N = 6250
E = 206250
D = 256
EF = 64
EPS = 1e-5
H0, F0 = 8, 32
H1, F1 = 4, 64

J = 14
SB = P * J
KSB = -(-E // SB)
KSB += KSB % 2
FRONT = KSB * SB - E
PAIRS = KSB // 2
assert 0 < FRONT < SB
W = D + 8
W1 = 2 * F1 + 2 * H1
NROWS = 6400
TILES = N // P
LAST0 = N - P
BIG = 1.0e30
NO_NODE = -1.0


def ge(eng, sem, value):
    if not isinstance(value, int) or value > 0:
        eng.wait_ge(sem, value)


def bc(ap, shape, *axes):
    for a in axes:
        ap = ap.unsqueeze(a)
    return ap.to_broadcast(shape)


class Chain:

    def __init__(self, eng, sem):
        self.eng, self.sem, self.base, self.n = eng, sem, 0, 0

    def start(self, base):
        self.base, self.n = base, 0

    def done(self, ins):
        self.n += 1
        ins.then_inc(self.sem, 1)
        return self.n

    def after(self, n=None):
        ge(self.eng, self.sem, self.base + (self.n if n is None else n))


def bank(nc, ctx, name, shape):
    size = 1
    for n in shape[1:]:
        size *= n
    whole = ctx.enter_context(nc.psum_tensor(name, [P, -(-size // 512) * 512], F32))
    view = whole[0:shape[0], 0:size]
    if len(shape) == 2:
        return view
    axes = "abcd"[:len(shape) - 1]
    return view.rearrange(f"p ({' '.join(axes)}) -> p {' '.join(axes)}", **dict(zip(axes, shape[1:])))


def make_identity(nc, pool, ident, sem):
    nc.gpsimd.memset(ident[:], 0.0).then_inc(sem, 1)
    pool.wait_ge(sem, 1)
    nc.gpsimd.affine_select(out=ident[:], in_=ident[:], compare_op=ALU.not_equal, fill=1.0, base=0,
                            pattern=[[-1, P]], channel_multiplier=1).then_inc(sem, 1)


def edge_tables(nc, src, dst, dst_f, src_pad, acc, adst, keep):
    with ExitStack() as ctx:
        def sb(name, shape, dt=F32):
            return ctx.enter_context(nc.sbuf_tensor(name, shape, dt))

        def sem(name):
            return ctx.enter_context(nc.semaphore(name))

        R = 125
        edges = sb("et_edges", [R, E // R], I32)
        edges_f = sb("et_edges_f", [R, E // R])
        pad_f = sb("et_pad_f", [1, FRONT + 1])
        pad_i = sb("et_pad_i", [1, FRONT], I32)
        zero = sb("et_zero", [P, W])
        ends_i = sb("et_ends_i", [1, 2 * KSB], I32)
        ends_f = sb("et_ends_f", [1, 2 * KSB])
        span_i = sb("et_span_i", [1, 2 * KSB], I32)
        span_f = sb("et_span_f", [1, 2 * KSB])
        ones = sb("et_ones", [1, KSB])
        ones_row = sb("et_ones_row", [1, P])
        rowid = sb("et_rowid", [P, 1])
        ends_ps = ctx.enter_context(nc.psum_tensor("et_ends_ps", [P, 2 * KSB], F32))
        s_dst = sem("et_dst")
        s_ends = sem("et_ends")
        s_set = sem("et_set")
        s_dve = sem("et_dve")
        s_pads = sem("et_pads")
        s_float = sem("et_float")
        s_bc = sem("et_bc")
        s_rowid = sem("et_rowid_sem")
        s_out = sem("et_out")
        block = ctx.enter_context(nc.Block())

        @block.sync
        def _(sp):
            sp.dma_start(edges[:], dst.rearrange("(p e) -> p e", p=R)).then_inc(s_dst, 16)
            sp.wait_ge(s_set, 1)
            with nc.allow_non_contiguous_dma(reason="one element per superblock"):
                body = dst[SB - FRONT:E]
                sp.dma_start(ends_i[:, 1:KSB], body.rearrange("(k e) -> k e", e=SB)[:, 0:1]
                             .rearrange("k e -> e k")).then_inc(s_ends, 16)
                sp.dma_start(ends_i[:, KSB + 1:2 * KSB], body.rearrange("(k e) -> k e", e=SB)[:, SB - 1:SB]
                             .rearrange("k e -> e k")).then_inc(s_ends, 16)
            sp.dma_start(ends_i[:, KSB:KSB + 1], dst[SB - FRONT - 1:SB - FRONT].unsqueeze(0)).then_inc(s_ends, 16)
            sp.dma_start(src_pad[FRONT:FRONT + E].rearrange("(p e) -> p e", p=R),
                         src.rearrange("(p e) -> p e", p=R)).then_inc(s_out, 16)
            sp.wait_ge(s_pads, 3)
            sp.dma_start(src_pad[0:FRONT].unsqueeze(0), pad_i[:]).then_inc(s_out, 16)
            sp.dma_start(dst_f[0:FRONT + 1].unsqueeze(0), pad_f[:]).then_inc(s_out, 16)
            sp.dma_start(dst_f[FRONT + 1 + E:FRONT + 1 + E + J + 1].unsqueeze(0), pad_f[:, 0:J + 1]).then_inc(s_out, 16)
            n_out = 4
            for a in acc:
                sp.dma_start(a.rearrange("(p r) c -> p r c", p=P),
                             bc(zero[:], [P, NROWS // P, W], 1)).then_inc(s_out, 16)
                n_out += 1
            sp.dma_start(adst[N:NROWS, :].rearrange("(p r) c -> p (r c)", p=50), zero[0:50, 0:3 * H0]).then_inc(s_out, 16)
            sp.wait_ge(s_float, 1)
            sp.dma_start(dst_f[FRONT + 1:FRONT + 1 + E].rearrange("(p e) -> p e", p=R), edges_f[:]).then_inc(s_out, 16)
            n_out += 2
            sp.wait_ge(s_out, 16 * n_out)

        @block.gpsimd
        def _(pool):
            nc.gpsimd.iota(rowid[:], pattern=[[0, 1]], base=0, channel_multiplier=1,
                           allow_small_or_imprecise_dtypes=True).then_inc(s_rowid, 1)

        @block.vector
        def _(dve):
            step = Chain(dve, s_dve)
            nc.vector.memset(ends_i[:], 0).then_inc(s_set, 1)
            nc.vector.memset(pad_f[:], NO_NODE).then_inc(s_pads, 1)
            nc.vector.memset(pad_i[:], 0).then_inc(s_pads, 1)
            nc.vector.memset(zero[:], 0.0).then_inc(s_pads, 1)
            step.done(nc.vector.memset(ones[:], 1.0))
            step.done(nc.vector.memset(ones_row[:], 1.0))
            step.done(nc.vector.memset(keep["win_i"][:], 0))
            dve.wait_ge(s_dst, 16)
            nc.vector.tensor_copy(edges_f[:], edges[:]).then_inc(s_float, 1)
            dve.wait_ge(s_ends, 48)
            step.done(nc.vector.tensor_copy(keep["base_i"][:], ends_i[:, 0:KSB]))
            step.done(nc.vector.tensor_copy(ends_f[:], ends_i[:]))
            step.after()
            step.done(nc.vector.tensor_tensor(span_i[:, 0:KSB], ends_i[:, KSB:2 * KSB], ends_i[:, 0:KSB], ALU.subtract))
            step.after()
            step.done(nc.vector.tensor_single_scalar(span_i[:, KSB:2 * KSB], span_i[:, 0:KSB], 7, op=ALU.arith_shift_right))
            step.after()
            step.done(nc.vector.tensor_copy(span_f[:, 0:KSB], span_i[:, KSB:2 * KSB]))
            step.after()
            step.done(nc.vector.tensor_scalar(span_f[:, KSB:2 * KSB], span_f[:, 0:KSB], 1.0, None, ALU.add))
            step.after()
            step.done(nc.vector.tensor_tensor_scan(span_f[:, 0:KSB], ones[:], span_f[:, KSB:2 * KSB], 0.0,
                                                   ALU.mult, ALU.add))
            step.after()
            step.done(nc.vector.tensor_copy(keep["win_i"][:, 1:KSB + 1], span_f[:, 0:KSB]))
            dve.wait_ge(s_bc, 1)
            dve.wait_ge(s_rowid, 1)
            step.done(nc.vector.tensor_copy(keep["base_f"][:], ends_ps[:, 0:KSB]))
            step.after()
            step.done(nc.vector.tensor_tensor(keep["last_rel"][:], ends_ps[:, KSB:2 * KSB], keep["base_f"][:], ALU.subtract))
            step.done(nc.vector.tensor_scalar(keep["minus_node"][:], keep["base_f"][:], rowid[:, 0:1], -1.0,
                                              ALU.add, ALU.mult))
            step.after()

        @block.tensor
        def _(pe):
            pe.wait_ge(s_dve, 5)
            nc.tensor.matmul(ends_ps[:], ones_row[:], ends_f[:], start=True, stop=True).then_inc(s_bc, 1)


def norm_tile(nc, dve, step, t, x_t, stats, mv, var_eps, std, rstd, h, s_var, s_std, s_gate):
    step.done(nc.vector.bn_stats(stats[:], x_t))
    step.after()
    dve.sem_inc(s_gate, 1)
    step.done(nc.vector.bn_aggr(mv[:], stats[:]))
    step.after()
    nc.vector.tensor_scalar(var_eps[:], mv[:, 1:2], EPS, None, ALU.add).then_inc(s_var, 1)
    dve.wait_ge(s_std, t + 1)
    step.done(nc.vector.reciprocal(rstd[:], std[:]))
    step.after()
    return nc.vector.tensor_scalar(h, x_t, mv[:, 0:1], rstd[:, 0:1], ALU.subtract, ALU.mult)


def node_stage(nc, layer, x, acc0, x1, table, adst, weights, identity):
    second = layer == 1
    cols = W + H0 if not second else W1
    width = W if not second else W1
    tag = f"n{layer}_"
    with ExitStack() as ctx:
        def sb(name, shape, dt=F32):
            return ctx.enter_context(nc.sbuf_tensor(tag + name, shape, dt))

        def sem(name):
            return ctx.enter_context(nc.semaphore(tag + name))

        def ps(name, shape):
            return bank(nc, ctx, tag + name, shape)

        ident = sb("ident", [P, P])
        rhs = sb("rhs", [P, 2, cols])
        x_in = [sb(f"x{s}", [P, D]) for s in range(2)]
        sums = [sb(f"sums{s}", [P, W]) for s in range(2)] if second else None
        x_new = [sb(f"x_new{s}", [P, D]) for s in range(2)] if second else x_in
        h = [sb(f"h{s}", [P, D]) for s in range(2)]
        hT = [sb(f"hT{s}", [P, 2, P]) for s in range(2)]
        row = [sb(f"row{s}", [P, cols]) for s in range(2)]
        stats = sb("stats", [P, nc.vector.BN_STATS_DIM])
        mv = sb("mv", [P, nc.vector.BN_AGGR_DIM])
        var_eps = sb("var_eps", [P, 1])
        std = sb("std", [P, 1])
        rstd = sb("rstd", [P, 1])
        den = sb("den", [P, H0])
        agg = sb("agg", [P, D])
        low = sb("low", [P, D])
        low_exp = sb("low_exp", [P, D])
        hT_ps = [ps(f"hT_ps{s}", [P, 2, P]) for s in range(2)]
        row_ps = [ps(f"row_ps{s}", [P, cols]) for s in range(2)]
        w_ps = ps("w_ps", [P, 512])
        if not second:
            w_in = sb("w_in", [P, 2, D])
            a_row = sb("a_row", [P, 3, D])
            we = sb("we", [P, D])
            prod = sb("prod", [P, D])
        else:
            w_in = sb("w_in", [F1, 2, D])
            a_row = sb("a_row", [F1, H1])

        s_id = sem("id")
        s_w = sem("w")
        s_wdve = sem("wdve")
        s_wps = sem("wps")
        s_rhs = sem("rhs_ready")
        s_x = [sem(f"x_in{s}") for s in range(2)]
        s_dve = sem("dve")
        s_low = sem("low_ready")
        s_exp = sem("exp_ready")
        s_new = sem("x_new_ready")
        s_var = sem("var_ready")
        s_gate = sem("gate")
        s_std = sem("std_ready")
        s_h = sem("h_ready")
        s_hTp = sem("hT_turned")
        s_hT = sem("hT_ready")
        s_rowp = sem("row_summed")
        s_row = sem("row_ready")
        s_st = [sem(f"stored{s}") for s in range(2)]
        block = ctx.enter_context(nc.Block())
        LOADS = 2 if second else 1
        STORES = 2

        def over_tiles(eng, body):
            for t in range(2):
                body(t, t, t * P)
            with eng.Fori(1, TILES // 2) as i:
                for s in range(2):
                    body(2 * i + s, s, (2 * i + s) * P)
            body(TILES, TILES % 2, LAST0)

        def use(t, s):
            return t // 2 + 1 if isinstance(t, int) else (t - s) // 2 + 1

        @block.sync
        def _(sp):
            if not second:
                sp.dma_start(w_in[:], weights["W"].rearrange("(c p) n -> p c n", p=P)).then_inc(s_w, 16)
                for n, a in enumerate(("a_src", "a_dst", "a_edge")):
                    sp.dma_start(a_row[:, n, :], bc(weights[a].rearrange("h f -> (h f)"), [P, D], 0)).then_inc(s_w, 16)
                for half in range(2):
                    sp.dma_start(we[EF * half:EF * half + EF, :], weights["We"]).then_inc(s_w, 16)
            else:
                sp.dma_start(w_in[:, 0, :], weights["Wf"]).then_inc(s_w, 16)
                sp.dma_start(w_in[:, 1, :], weights["Wr"]).then_inc(s_w, 16)
                with nc.allow_non_contiguous_dma(reason="256 weights, turned"):
                    sp.dma_start(a_row[:], weights["attn"][0].rearrange("h f -> f h")).then_inc(s_w, 16)

            def load(t, s, r0):
                ge(sp, s_h, t - 1)
                sp.dma_start(x_in[s][:], x[bass.ds(r0, P), :]).then_inc(s_x[s], 16)
                if second:
                    sp.dma_start(sums[s][:], acc0[bass.ds(r0, P), :]).then_inc(s_x[s], 16)

            over_tiles(sp, load)

        @block.gpsimd
        def _(pool):
            make_identity(nc, pool, ident, s_id)

        @block.vector
        def _(dve):
            step = Chain(dve, s_wdve)
            if not second:
                dve.wait_ge(s_w, 96)
                step.done(nc.vector.memset(identity["edge_w"][:], 0.0))
                for c in range(2):
                    nc.vector.tensor_copy(rhs[:, c, 0:D], w_in[:, c, :]).then_inc(s_rhs, 1)
                    for n in range(2):
                        step.after()
                        step.done(nc.vector.tensor_tensor(prod[:], w_in[:, c, :], a_row[:, n, :], ALU.mult))
                        step.after()
                        step.done(nc.vector.tensor_reduce(rhs[:, c, D + n * H0:D + (n + 1) * H0],
                                                          prod[:].rearrange("p (h f) -> p h f", h=H0), AX_X, ALU.add))
                step.after()
                step.done(nc.vector.tensor_tensor(prod[:], we[:], a_row[:, 2, :], ALU.mult))
                step.after()
                for half in range(2):
                    q = slice(EF * half, EF * half + EF)
                    step.done(nc.vector.tensor_reduce(identity["edge_w"][q, H0 * half:H0 * half + H0],
                                                      prod[q, :].rearrange("p (h f) -> p h f", h=H0), AX_X, ALU.add))
                step.after()
                nc.vector.memset(rstd[:], 0.0).then_inc(s_rhs, 1)
            else:
                for c in range(2):
                    dve.wait_ge(s_wps, 2)
                    nc.vector.tensor_copy(rhs[:, c, :], w_ps[:, c * W1:(c + 1) * W1]).then_inc(s_rhs, 1)
                nc.vector.memset(rstd[:], 0.0).then_inc(s_rhs, 1)
            steps = 3 + (6 if second else 0)
            tile = Chain(dve, s_dve)

            def body(t, s, r0):
                tile.start(t * steps)
                dve.wait_ge(s_x[s], 16 * LOADS * use(t, s))
                if second:
                    heads = lambda ap: ap.rearrange("p (h f) -> p h f", h=H0)
                    tile.done(nc.vector.tensor_scalar(den[:], sums[s][:, D:D + H0], 1e-30, None, ALU.max))
                    tile.after()
                    tile.done(nc.vector.reciprocal(den[:], den[:]))
                    tile.after()
                    tile.done(nc.vector.tensor_tensor(heads(agg[:]), heads(sums[s][:, 0:D]),
                                                      bc(den[:], [P, H0, F0], 2), ALU.mult))
                    tile.after()
                    ge(dve, s_exp, t)
                    nc.vector.tensor_scalar(low[:], agg[:], 0.0, None, ALU.min).then_inc(s_low, 1)
                    tile.done(nc.vector.tensor_scalar(agg[:], agg[:], 0.0, -1.0, ALU.max, ALU.add))
                    tile.after()
                    tile.done(nc.vector.tensor_tensor(agg[:], agg[:], x_in[s][:], ALU.add))
                    tile.after()
                    dve.wait_ge(s_exp, t + 1)
                    ge(dve, s_st[s], 16 * STORES * (use(t, s) - 1))
                    tile.done(nc.vector.tensor_tensor(x_new[s][:], agg[:], low_exp[:], ALU.add))
                    tile.after()
                ge(dve, s_hTp, t - 1)
                norm_tile(nc, dve, tile, t, x_new[s][:], stats, mv, var_eps, std, rstd, h[s][:], s_var, s_std, s_gate).then_inc(s_h, 1)

            over_tiles(dve, body)

        @block.tensor
        def _(pe):
            pe.wait_ge(s_id, 2)
            if second:
                pe.wait_ge(s_w, 48)
                for c in range(2):
                    cs = slice(c * P, (c + 1) * P)
                    o = c * W1
                    for n in range(2):
                        nc.tensor.transpose(w_ps[:, o + n * F1:o + (n + 1) * F1], w_in[:, n, cs], ident[0:F1, 0:F1])
                        last = nc.tensor.matmul(w_ps[:, o + 2 * F1 + n * H1:o + 2 * F1 + (n + 1) * H1],
                                                w_in[:, n, cs], a_row[:], start=True, stop=True)
                    last.then_inc(s_wps, 1)
            pe.wait_ge(s_rhs, 3)

            def body(t, s, r0):
                pe.wait_ge(s_h, t + 1)
                ge(pe, s_hT, t - 1)
                for c in range(2):
                    last = nc.tensor.transpose(hT_ps[s][:, c, :], h[s][:, c * P:(c + 1) * P], ident[:])
                last.then_inc(s_hTp, 1)
                pe.wait_ge(s_hT, t + 1)
                ge(pe, s_row, t - 1)
                for c in range(2):
                    last = nc.tensor.matmul(row_ps[s], hT[s][:, c, :], rhs[:, c, :], start=(c == 0), stop=(c == 1))
                last.then_inc(s_rowp, 1)

            over_tiles(pe, body)

        @block.scalar
        def _(act):
            def body(t, s, r0):
                if second:
                    act.wait_ge(s_low, t + 1)
                    ge(act, s_dve, t * 9)
                    nc.scalar.activation(low_exp[:], low[:], ACT.Exp).then_inc(s_exp, 1)
                act.wait_ge(s_var, t + 1)
                nc.scalar.activation(std[:], var_eps[:], ACT.Sqrt).then_inc(s_std, 1)
                act.wait_ge(s_hTp, t + 1)
                ge(act, s_rowp, t - 1)
                nc.scalar.activation(hT[s][:], hT_ps[s], ACT.Relu).then_inc(s_hT, 1)
                act.wait_ge(s_rowp, t + 1)
                ge(act, s_st[s], 16 * STORES * (use(t, s) - 1))
                nc.scalar.copy(row[s][:], row_ps[s]).then_inc(s_row, 1)
                if isinstance(t, int) and t == TILES:
                    act.wait_ge(s_st[1 - s], 16 * STORES * ((TILES + 1) // 2))
                act.wait_ge(s_row, t + 1)
                act.dma_start(table[bass.ds(r0, P), :], row[s][:, 0:width]).then_inc(s_st[s], 16)
                if second:
                    act.dma_start(x1[bass.ds(r0, P), :], x_new[s][:]).then_inc(s_st[s], 16)
                else:
                    act.dma_start(adst[bass.ds(r0, P), :], row[s][:, W:W + H0]).then_inc(s_st[s], 16)

            
            over_tiles(act, body)
            act.wait_ge(s_st[0], 16 * STORES * (TILES // 2 + 1))
            act.wait_ge(s_st[1], 16 * STORES * (TILES // 2))


def edge_stage(nc, layer, table, dst_f, src_pad, attr, adst, acc, keep, gmax):
    first_layer = layer == 0
    H = H0 if first_layer else H1
    TW = W if first_layer else W1
    HJ = H * J
    AF = EF if first_layer else 2
    tag = f"e{layer}_"
    with ExitStack() as ctx:
        def sb(name, shape, dt=F32):
            return ctx.enter_context(nc.sbuf_tensor(tag + name, shape, dt))

        def sem(name):
            return ctx.enter_context(nc.semaphore(tag + name))

        def ps(name, shape):
            return bank(nc, ctx, tag + name, shape)

        ident = sb("ident", [P, P])
        iota = sb("iota", [P, P])
        rowid = sb("rowid", [P, 1])
        zero_row = sb("zero_row", [1, P])
        idx = [sb(f"idx{s}", [P, J], I32) for s in range(2)]
        dwin = [sb(f"dwin{s}", [P, J + 2]) for s in range(2)]
        att = [sb(f"att{s}", [P, J, AF]) for s in range(2)]
        rows = [sb(f"rows{s}", [P, J, TW]) for s in range(2)]
        drel = sb("drel", [P, J + 1])
        last_rel = sb("last_rel", [P, 1])
        headmask = sb("headmask", [P, J])
        tailmask = sb("tailmask", [P, J])
        cut = sb("cut", [P, J + 1])
        link = sb("link", [P, HJ + 1])
        score = sb("score", [P, H, J])
        fwd = sb("fwd", [P, H, J])
        bwd = sb("bwd", [P, H, J])
        edge_links = sb("edge_links", [P, 2, H])
        links_T = sb("links_T", [H, 2, P])
        fwd_T = sb("fwd_T", [H, P + 1])
        bwd_T = sb("bwd_T", [H, P + 1])
        local = sb("local", [P, H, J])
        from_prev = sb("from_prev", [P, H, J])
        from_next = sb("from_next", [P, H, J])
        top = sb("top", [P, H, J])
        old = sb("old", [P, H])
        z = sb("z", [P, H, J])
        z_old = sb("z_old", [P, H])
        fade = sb("fade", [P, H])
        msg = sb("msg", [P, J, W])
        onehot = sb("onehot", [P, J, P])
        onehot_carry = sb("onehot_carry", [1, P])
        pick_last = sb("pick_last", [P, 1])
        carry = sb("carry", [1, W])
        out_rows = sb("out_rows", [P, W])

        sums_ps = ps("sums_ps", [P, W])
        ends_ps = ps("ends_ps", [H, 4, P])
        back_ps = ps("back_ps", [P, 2, H])
        carry_ps = ps("carry_ps", [1, W])
        if first_layer:
            both = sb("both", [P, 2, H, J])
            both_l = sb("both_l", [P, 2, H, J])
            old_l = sb("old_l", [P, H])
            att_T = sb("att_T", [P, J // 2, P])
            dst_bc = [sb(f"dst_bc{s}", [P, SB]) for s in range(2)]
            dist = sb("dist", [P, SB])
            node_hot = sb("node_hot", [P, SB])
            minus_node = sb("minus_node", [P, 1])
            adst_win = sb("adst_win", [P, H0])
            att_ps = ps("att_ps", [P, 8, P])
            ae_ps = ps("ae_ps", [P, J, H0])
            ad_ps = ps("ad_ps", [P, J, H0])
            edge_w = keep["edge_w"]
            edge_score = [sb(f"edge_score{s}", [P, J, H0]) for s in range(2)]
            node_score = [sb(f"node_score{s}", [P, J, H0]) for s in range(2)]
        else:
            t0 = sb("t0", [P, H, J])
            t1 = sb("t1", [P, H, J])
            t2 = sb("t2", [P, H, J])
            kmax = sb("kmax", [P, H])
            m0 = sb("m0", [P, J, F1])
            m1 = sb("m1", [P, J, F1])
            m2 = sb("m2", [P, J, F1])

        s_setup = sem("setup")
        s_pool_setup = sem("pool_setup")
        s_idx = [sem(f"idx_in{s}") for s in range(2)]
        s_dwin = [sem(f"dwin_in{s}") for s in range(2)]
        s_att = [sem(f"att_in{s}") for s in range(2)]
        s_dstbc = [sem(f"dst_bc_in{s}") for s in range(2)]
        s_adw = sem("adst_win_in")
        s_go = sem("slot_granted")
        s_gate = sem("gate")
        s_rows = [sem(f"rows_in{s}") for s in range(2)]
        s_rows_used = sem("rows_used")
        s_dwin_used = sem("dwin_used")
        s_att_used = sem("att_used")
        s_dstbc_used = sem("dst_bc_used")
        s_dve = sem("dve")
        s_links_T = sem("links_T_ready")
        s_ends = sem("ends_turned")
        s_T = sem("scans_T_ready")
        s_back = sem("back_turned")
        s_z = sem("z_ready")
        s_exp = sem("exp_ready")
        s_msg = sem("msg_ready")
        s_hot = sem("onehot_ready")
        s_mm = sem("window_summed")
        s_out = sem("out_rows_ready")
        s_carry = sem("carry_picked")
        s_stored = sem("stored")
        s_out_free = sem("out_rows_stored")
        s_act = sem("act")
        s_node_hot = sem("node_hot_ready")
        s_spread = sem("adst_spread")
        s_ad = sem("ad_ready")
        s_attp = sem("att_turned")
        s_attT = sem("att_T_ready")
        s_ae = sem("ae_ready")
        s_edge_score = sem("edge_score_ready")
        s_node_score = sem("node_score_ready")
        block = ctx.enter_context(nc.Block())
        STEPS = 26 if first_layer else 31
        first_scan = 11 if first_layer else 14

        def over_superblocks(eng, body):
            for s in range(2):
                body(s, s, 2)
            with eng.Fori(1, PAIRS - 1) as i:
                for s in range(2):
                    body(2 * i + s, s, 2)
            for s in range(2):
                body(KSB - 2 + s, s, 1 - s)

        def use(k, s):
            return k // 2 + 1 if isinstance(k, int) else (k - s) // 2 + 1

        def windows(eng, k):
            lo = eng.value_load(keep["win_i"][0:1, bass.ds(k, 1)], min_val=0, max_val=KSB + N // P + 1)
            hi = eng.value_load(keep["win_i"][0:1, bass.ds(k + 1, 1)], min_val=1, max_val=KSB + N // P + 1)
            return lo, hi

        def window_row(eng, base, w, lo):
            return nc.s_assert_within(eng.snap(base + (w - lo) * P), 0, NROWS - P, skip_runtime_bounds_check_because=
                                      "a window begins at or before its superblock's last destination")

        @block.sync
        def _(sp):
            def load(k, s):
                n = use(k, s)
                e0 = SB * k
                ge(sp, s_rows[s], 16 * J * (n - 1))
                sp.dma_start(idx[s][:], src_pad[bass.ds(e0, SB)].rearrange("(p j) -> p j", p=P)).then_inc(s_idx[s], 16)
                ge(sp, s_dwin_used, k - 1)
                sp.dma_start(dwin[s][:, 0:J], dst_f[bass.ds(e0, SB)].rearrange("(p j) -> p j", p=P))\
                  .then_inc(s_dwin[s], 16)
                sp.dma_start(dwin[s][:, J:J + 2], dst_f[bass.ds(e0 + J, SB)].rearrange("(p j) -> p j", p=P)[:, 0:2])\
                  .then_inc(s_dwin[s], 16)
                ge(sp, s_att_used, k - 1)
                if isinstance(k, int) and k == 0:
                    p0, j0 = FRONT // J, FRONT % J
                    part = J - j0
                    sp.wait_ge(s_setup, 1)
                    sp.dma_start(att[s][p0:p0 + 1, j0:J, :], attr[0:part, :].unsqueeze(0)).then_inc(s_att[s], 8 * 2)
                    sp.dma_start(att[s][p0 + 1:P, :, :], attr[part:SB - FRONT, :].rearrange("(p j) c -> p j c", j=J))\
                      .then_inc(s_att[s], 16)
                else:
                    sp.dma_start(att[s][:], attr[bass.ds(e0 - FRONT, SB), :].rearrange("(p j) c -> p j c", j=J))\
                      .then_inc(s_att[s], 16)
                if first_layer:
                    ge(sp, s_dstbc_used, k - 1)
                    sp.dma_start(dst_bc[s][:], bc(dst_f[bass.ds(e0 + 1, SB)], [P, SB], 0)).then_inc(s_dstbc[s], 16)

            def load_adst(k):
                base = sp.value_load(keep["base_i"][0:1, bass.ds(k, 1)], min_val=0, max_val=N - 1)
                lo, hi = windows(sp, k)
                with sp.Fori(lo, hi) as w:
                    sp.wait_ge(s_spread, w + 1)
                    sp.dma_start(adst_win[:], adst[bass.ds(window_row(sp, base, w, lo), P), :])\
                      .then_inc(s_adw, 16)

            sp.sem_inc(s_spread, 1)
            sp.sem_inc(s_out_free, 1)
            load(0, 0)
            load(1, 1)
            if first_layer:
                load_adst(0)

            def body(k, s, ahead):
                if first_layer and ahead:
                    load_adst(k + 1)
                if ahead == 2:
                    load(k + 2, s)
                base = sp.value_load(keep["base_i"][0:1, bass.ds(k, 1)], min_val=0, max_val=N - 1)
                lo, hi = windows(sp, k)
                with sp.Fori(lo, hi) as w:
                    sp.wait_ge(s_out, w + 1)
                    sp.dma_start(acc[bass.ds(window_row(sp, base, w, lo), P), :], out_rows[:])\
                      .then_inc(s_stored, 16)
                    sp.wait_ge(s_stored, 16 * w + 16)
                    sp.sem_inc(s_out_free, 1)

            over_superblocks(sp, body)

        @block.gpsimd
        def _(pool):
            make_identity(nc, pool, ident, s_pool_setup)
            nc.gpsimd.iota(iota[:], pattern=[[1, P]], base=0, channel_multiplier=0,
                           allow_small_or_imprecise_dtypes=True).then_inc(s_pool_setup, 1)
            nc.gpsimd.iota(rowid[:], pattern=[[0, 1]], base=0, channel_multiplier=1,
                           allow_small_or_imprecise_dtypes=True).then_inc(s_pool_setup, 1)

            def body(k, s, ahead):
                n = use(k, s)
                pool.wait_ge(s_idx[s], 16 * n)
                ge(pool, s_rows_used, k - 1)
                pool.sem_inc(s_go, 1)
                for j in range(J):
                    pool.indirect_dma_start(rows[s][:, j, :], None, table[:, :],
                                            bass.IndirectOffsetOnAxis(ap=idx[s][:, j:j + 1], axis=0))\
                        .then_inc(s_rows[s], 16)

            over_superblocks(pool, body)
            if not first_layer:
                pool.wait_ge(s_msg, KSB)
                nc.gpsimd.partition_all_reduce(gmax[:], keep["gmax_part"][:], P, bass.bass_isa.ReduceOp.max)\
                    .then_inc(s_go, 1)
                pool.wait_ge(s_go, KSB + 1)

        @block.vector
        def _(dve):
            nc.vector.memset(link[:], -BIG).then_inc(s_dve, 1)
            nc.vector.memset(fwd_T[:], -BIG).then_inc(s_dve, 1)
            nc.vector.memset(bwd_T[:], -BIG).then_inc(s_dve, 1)
            nc.vector.memset(zero_row[:], 0.0).then_inc(s_dve, 1)
            nc.vector.memset(carry[:], 0.0).then_inc(s_dve, 1)
            nc.vector.memset(att[0][:], 0.0).then_inc(s_setup, 1)
            SETUP = 5
            dve.wait_ge(s_dve, SETUP)
            dve.wait_ge(s_pool_setup, 4)
            c = Chain(dve, s_dve)
            V = nc.vector

            def body(k, s, ahead):
                n = use(k, s)
                lo, hi = windows(dve, k)
                c.start(SETUP + k * STEPS)
                dw = dwin[s]
                dve.wait_ge(s_dwin[s], 32 * n)
                c.done(V.tensor_scalar(drel[:], dw[:, 0:J + 1], keep["base_f"][:, bass.ds(k, 1)], None, ALU.subtract))
                c.done(V.tensor_copy(last_rel[:], keep["last_rel"][:, bass.ds(k, 1)]))
                c.done(V.tensor_scalar(headmask[:], dw[:, 1:J + 1], dw[:, 0:1], -BIG, ALU.not_equal, ALU.mult))
                c.done(V.tensor_scalar(tailmask[:], dw[:, 1:J + 1], dw[:, J + 1:J + 2], -BIG, ALU.not_equal, ALU.mult))
                c.done(V.tensor_tensor(cut[:], dw[:, 1:J + 2], dw[:, 0:J + 1], ALU.not_equal))
                c.after()
                c.done(V.tensor_scalar(link[:, 0:HJ].rearrange("p (h j) -> p h j", h=H)[:, :, 1:J],
                                       bc(cut[:, 1:J], [P, H, J - 1], 1), -BIG, None, ALU.mult))
                c.done(V.tensor_copy(edge_links[:, 0, :], headmask[:, J - 1:J].to_broadcast([P, H])))
                c.done(V.tensor_copy(edge_links[:, 1, :], tailmask[:, 0:1].to_broadcast([P, H])))
                dve.wait_ge(s_rows[s], 16 * J * n)
                if first_layer:
                    dve.wait_ge(s_edge_score, k + 1)
                    c.done(V.tensor_tensor(score[:], rows[s][:, :, D:D + H].rearrange("p j h -> p h j"),
                                           edge_score[s][:].rearrange("p j h -> p h j"), ALU.add))
                else:
                    dve.wait_ge(s_att[s], 16 * n + 16 if s == 0 else 16 * n)
                    up = rows[s][:, :, 2 * F1:2 * F1 + 2 * H1].rearrange("p j (d h) -> p d h j", d=2)
                    c.done(V.tensor_tensor(t0[:], up[:, 0], bc(att[s][:, :, 0], [P, H, J], 1), ALU.mult))
                    c.done(V.tensor_tensor(t1[:], up[:, 1], bc(att[s][:, :, 1], [P, H, J], 1), ALU.mult))
                    c.after()
                    c.done(V.tensor_tensor(t2[:], t0[:], t1[:], ALU.add))
                    c.after()
                    c.done(V.scalar_tensor_tensor(score[:], t2[:], 0.2, t2[:], ALU.mult, ALU.max))
                c.after()
                flat = lambda t: t[:].rearrange("p h j -> p (h j)")
                c.done(V.tensor_tensor_scan(flat(fwd), link[:, 0:HJ], flat(score), -BIG, ALU.add, ALU.max))
                ends = c.done(V.tensor_tensor_scan(flat(bwd)[:, ::-1], link[:, 1:HJ + 1][:, ::-1], flat(score)[:, ::-1],
                                                   -BIG, ALU.add, ALU.max))
                c.done(V.tensor_copy(fwd_T[:, 0:1], fwd_T[:, P:P + 1]))
                c.after(ends)
                c.done(V.tensor_tensor(local[:], fwd[:], bwd[:], ALU.max))
                if not first_layer:
                    c.after()
                    if isinstance(k, int) and k == 0:
                        c.done(V.tensor_scalar(t0[:, 0, :], dw[:, 1:J + 1], NO_NODE, -BIG, ALU.is_equal, ALU.mult))
                        c.after()
                        c.done(V.tensor_tensor(t1[:], score[:], bc(t0[:, 0, :], [P, H, J], 1), ALU.add))
                        c.after()
                        c.done(V.tensor_reduce(keep["gmax_part"][:], t1[:], AX_X, ALU.max))
                        c.after()
                    else:
                        c.done(V.tensor_reduce(kmax[:], score[:], AX_X, ALU.max))
                        c.after()
                        c.done(V.tensor_tensor(keep["gmax_part"][:], keep["gmax_part"][:], kmax[:], ALU.max))
                        c.done(V.memset(t0[:, 0, 0:1], 0.0))
                dve.wait_ge(s_links_T, k + 1)
                dve.wait_ge(s_ends, k + 1)
                c.after()
                c.done(V.tensor_tensor_scan(fwd_T[:, 1:P + 1], links_T[:, 0, :], ends_ps[:, 0, :], fwd_T[:, 0:1],
                                            ALU.add, ALU.max))
                V.tensor_tensor_scan(bwd_T[:, 0:P][:, ::-1], links_T[:, 1, :][:, ::-1], ends_ps[:, 1, :][:, ::-1],
                                     -BIG, ALU.add, ALU.max).then_inc(s_T, 1)
                dve.wait_ge(s_back, k + 1)
                hj = [P, H, J]
                c.done(V.tensor_tensor(from_prev[:], bc(headmask[:], hj, 1), bc(back_ps[:, 0, :], hj, 2), ALU.add))
                c.done(V.tensor_tensor(from_next[:], bc(tailmask[:], hj, 1), bc(back_ps[:, 1, :], hj, 2), ALU.add))
                c.after()
                c.done(V.tensor_tensor(top[:], from_prev[:], from_next[:], ALU.max))
                c.after()
                if first_layer:
                    dve.wait_ge(s_node_score, k + 1)
                    c.done(V.tensor_tensor(top[:], top[:], local[:], ALU.max))
                    ad = node_score[s][:].rearrange("p j h -> p h j")
                    c.done(V.tensor_tensor(both[:, 0], score[:], ad, ALU.add))
                    c.done(V.tensor_tensor(old[:], from_prev[:, :, 0], ad[:, :, 0], ALU.add))
                    c.after()
                    c.done(V.tensor_tensor(both[:, 1], top[:], ad, ALU.add))
                    c.after()
                    c.done(V.scalar_tensor_tensor(both_l[:], both[:], 0.01, both[:], ALU.mult, ALU.max))
                    c.done(V.scalar_tensor_tensor(old_l[:], old[:], 0.01, old[:], ALU.mult, ALU.max))
                    c.after()
                    score_l, top_l, old_v = both_l[:, 0], both_l[:, 1], old_l[:]
                else:
                    c.done(V.tensor_tensor(top[:], top[:], local[:], ALU.max))
                    c.after()
                    score_l, top_l, old_v = score[:], top[:], from_prev[:, :, 0]
                ge(dve, s_exp, 2 * k)
                V.tensor_tensor(z[:], score_l, top_l, ALU.subtract).then_inc(s_z, 1)
                V.tensor_tensor(z_old[:], old_v, top_l[:, :, 0], ALU.subtract).then_inc(s_z, 1)
                dve.wait_ge(s_exp, 2 * k + 2)
                if first_layer:
                    c.done(V.tensor_tensor(msg[:, :, 0:D].rearrange("p j (h f) -> p j h f", h=H),
                                           rows[s][:, :, 0:D].rearrange("p j (h f) -> p j h f", h=H),
                                           bc(msg[:, :, D:D + H], [P, J, H, F0], 3), ALU.mult))
                else:
                    c.done(V.tensor_tensor(m0[:], rows[s][:, :, 0:F1], bc(att[s][:, :, 0], [P, J, F1], 2), ALU.mult))
                    c.done(V.tensor_tensor(m1[:], rows[s][:, :, F1:2 * F1], bc(att[s][:, :, 1], [P, J, F1], 2), ALU.mult))
                    c.after()
                    c.done(V.tensor_tensor(m2[:], m0[:], m1[:], ALU.add))
                    c.done(V.tensor_tensor(msg[:, :, D + H:W].rearrange("p j h -> p h j"), top[:],
                                           bc(cut[:, 1:J + 1], hj, 1), ALU.mult))
                    c.after()
                    c.done(V.tensor_tensor(msg[:, :, 0:D].rearrange("p j (h f) -> p j h f", h=H),
                                           bc(m2[:], [P, J, H, F1], 2), bc(msg[:, :, D:D + H], [P, J, H, F1], 3),
                                           ALU.mult))
                dve.wait_ge(s_carry, lo + 1)
                if isinstance(k, int) and k == 0:
                    c.done(V.memset(carry[:, 0:D], 0.0))
                    c.done(V.memset(carry[:, D:W], 0.0))
                else:
                    c.done(V.tensor_tensor(carry[:, 0:D].rearrange("p (h f) -> p h f", h=H),
                                           carry_ps[:, 0:D].rearrange("p (h f) -> p h f", h=H),
                                           bc(fade[0:1, :], [1, H, D // H], 2), ALU.mult))
                    c.done(V.tensor_tensor(carry[:, D:W].rearrange("p (g h) -> p g h", h=H),
                                           carry_ps[:, D:W].rearrange("p (g h) -> p g h", h=H),
                                           bc(fade[0:1, :], [1, 8 // H, H], 1), ALU.mult))
                c.after()
                for sm in (s_rows_used, s_dwin_used, s_msg) + (() if first_layer else (s_att_used,)):
                    dve.sem_inc(sm, 1)
                assert c.n == STEPS, (layer, c.n)
                with dve.Fori(lo, hi) as w:
                    dve.wait_ge(s_mm, w + 1)
                    V.tensor_tensor(onehot[:], bc(iota[:], [P, J, P], 1), bc(drel[:, 1:J + 1], [P, J, P], 2),
                                    ALU.is_equal).then_inc(s_hot, 1)
                    V.tensor_scalar(onehot_carry[:], iota[0:1, :], drel[0:1, 0:1], None, ALU.is_equal).then_inc(s_hot, 1)
                    V.tensor_tensor(pick_last[:], rowid[:], last_rel[:], ALU.is_equal).then_inc(s_hot, 1)
                    dve.wait_ge(s_hot, 5 * w + 3)
                    V.tensor_scalar(drel[:], drel[:], -float(P), None, ALU.add).then_inc(s_hot, 1)
                    V.tensor_scalar(last_rel[:], last_rel[:], -float(P), None, ALU.add).then_inc(s_hot, 1)
                    dve.wait_ge(s_hot, 5 * w + 5)

            over_superblocks(dve, body)

        @block.scalar
        def _(act):
            a = Chain(act, s_act)

            def ahead_work(k, s):
                n = use(k, s)
                lo, hi = windows(act, k)
                act.wait_ge(s_dstbc[s], 16 * n)
                nc.scalar.copy(minus_node[:], keep["minus_node"][:, bass.ds(k, 1)]).then_inc(s_act, 1)
                act.wait_ge(s_act, lo * 3 + (k + 1))
                with act.Fori(lo, hi) as w:
                    base = act.snap(w * 3 + (k + 1))
                    nc.scalar.activation(dist[:], dst_bc[s][:], ACT.Abs, bias=minus_node[:, 0:1]).then_inc(s_act, 1)
                    act.wait_ge(s_act, base + 1)
                    act.wait_ge(s_spread, w + 1)
                    nc.scalar.activation(node_hot[:], dist[:], ACT.Relu, bias=1.0, scale=-1.0).then_inc(s_node_hot, 1)
                    nc.scalar.activation(minus_node[:], minus_node[:], ACT.Copy, bias=-float(P)).then_inc(s_act, 1)
                    act.wait_ge(s_node_hot, w + 1)
                    act.wait_ge(s_act, base + 2)
                    act.sem_inc(s_act, 1)
                act.sem_inc(s_dstbc_used, 1)
                act.wait_ge(s_attp, k + 1)
                ge(act, s_ae, k)
                nc.scalar.copy(att_T[:], att_ps[:, 0:J // 2, :]).then_inc(s_attT, 1)
                ge(act, s_msg, k - 1)
                act.wait_ge(s_ad, k + 1)
                nc.scalar.copy(node_score[s][:], ad_ps).then_inc(s_node_score, 1)
                act.wait_ge(s_ae, k + 1)
                nc.scalar.copy(edge_score[s][:], ae_ps).then_inc(s_edge_score, 1)

            if first_layer:
                ahead_work(0, 0)

            def body(k, s, ahead):
                lo, hi = windows(act, k)
                act.wait_ge(s_ends, k + 1)
                nc.scalar.copy(links_T[:], ends_ps[:, 2:4, :]).then_inc(s_links_T, 1)
                act.wait_ge(s_z, 2 * k + 2)
                act.wait_ge(s_mm, lo + 1)
                ge(act, s_msg, k)
                nc.scalar.activation(msg[:, :, D:D + H].rearrange("p j h -> p h j"), z[:], ACT.Exp).then_inc(s_exp, 1)
                nc.scalar.activation(fade[:], z_old[:], ACT.Exp).then_inc(s_exp, 1)
                if first_layer and ahead:
                    ahead_work(k + 1, 1 - s)
                with act.Fori(lo, hi) as w:
                    act.wait_ge(s_mm, w + 2)
                    act.wait_ge(s_out_free, w + 1)
                    act.wait_ge(s_carry, w + 1)
                    nc.scalar.copy(out_rows[:], sums_ps).then_inc(s_out, 1)

            over_superblocks(act, body)

        @block.tensor
        def _(pe):
            pe.wait_ge(s_pool_setup, 4)
            pe.wait_ge(s_dve, 5)
            pe.sem_inc(s_mm, 1)
            pe.sem_inc(s_carry, 1)

            def ahead_work(k, s):
                n = use(k, s)
                lo, hi = windows(pe, k)
                flat = ad_ps.rearrange("p j h -> p (j h)")
                ge(pe, s_node_score, k)
                nc.tensor.matmul(flat, zero_row[:], zero_row[:, 0:HJ], start=True, stop=False, skip_group_check=True)
                with pe.Fori(lo, hi) as w:
                    pe.wait_ge(s_node_hot, w + 1)
                    pe.wait_ge(s_adw, 16 * w + 16)
                    hot = node_hot[:].rearrange("p (e j) -> p j e", j=J)
                    for j in range(J):
                        last = nc.tensor.matmul(ad_ps[:, j, :], hot[:, j, :], adst_win[:], start=False, stop=False,
                                                skip_group_check=True)
                    last.then_inc(s_spread, 1)
                nc.tensor.matmul(flat, zero_row[:], zero_row[:, 0:HJ], start=False, stop=True, skip_group_check=True)\
                    .then_inc(s_ad, 1)
                pe.wait_ge(s_att[s], 16 * n + 16 if s == 0 else 16 * n)
                ge(pe, s_attT, k)
                for q in range(J // 2):
                    last = nc.tensor.transpose(att_ps[:, q, :], att[s][:, 2 * q:2 * q + 2, :].rearrange("p j c -> p (j c)"),
                                               ident[:])
                last.then_inc(s_attp, 1)
                pe.wait_ge(s_attT, k + 1)
                ge(pe, s_edge_score, k)
                for q in range(J // 2):
                    last = nc.tensor.matmul(ae_ps[:, 2 * q:2 * q + 2, :].rearrange("p j h -> p (j h)"),
                                            att_T[:, q, :], edge_w[:], start=True, stop=True)
                last.then_inc(s_ae, 1)
                pe.sem_inc(s_att_used, 1)

            if first_layer:
                ahead_work(0, 0)

            def body(k, s, ahead):
                lo, hi = windows(pe, k)
                pe.wait_ge(s_dve, 5 + k * STEPS + first_scan)
                nc.tensor.transpose(ends_ps[:, 0, :], fwd[:, :, J - 1], ident[:])
                nc.tensor.transpose(ends_ps[:, 1, :], bwd[:, :, 0], ident[:])
                nc.tensor.transpose(ends_ps[:, 2, :], edge_links[:, 0, :], ident[:])
                nc.tensor.transpose(ends_ps[:, 3, :], edge_links[:, 1, :], ident[:]).then_inc(s_ends, 1)
                pe.wait_ge(s_T, k + 1)
                pe.wait_ge(s_dve, 5 + k * STEPS + first_scan + (3 if first_layer else 6))
                pe.sem_inc(s_gate, 1)
                nc.tensor.transpose(back_ps[:, 0, :], fwd_T[:, 0:P], ident[0:H, 0:H])
                nc.tensor.transpose(back_ps[:, 1, :], bwd_T[:, 1:P + 1], ident[0:H, 0:H]).then_inc(s_back, 1)
                if first_layer and ahead:
                    ahead_work(k + 1, 1 - s)
                with pe.Fori(lo, hi) as w:
                    pe.wait_ge(s_msg, k + 1)
                    pe.wait_ge(s_hot, 5 * w + 3)
                    pe.wait_ge(s_out_free, w + 1)
                    for j in range(J):
                        nc.tensor.matmul(sums_ps, onehot[:, j, :], msg[:, j, :], start=(j == 0), stop=False)
                    nc.tensor.matmul(sums_ps, onehot_carry[:], carry[:], start=False, stop=True).then_inc(s_mm, 1)
                    pe.wait_ge(s_out, w + 1)
                    nc.tensor.matmul(carry_ps, pick_last[:], out_rows[:], start=True, stop=True).then_inc(s_carry, 1)

            over_superblocks(pe, body)


def final_stage(nc, x1, acc, gmax, out):
    with ExitStack() as ctx:
        def sb(name, shape, dt=F32):
            return ctx.enter_context(nc.sbuf_tensor("f_" + name, shape, dt))

        def sem(name):
            return ctx.enter_context(nc.semaphore("f_" + name))

        x_in = [sb(f"x{s}", [P, D]) for s in range(2)]
        sums = [sb(f"sums{s}", [P, W]) for s in range(2)]
        y = [sb(f"y{s}", [P, D]) for s in range(2)]
        gap = sb("gap", [P, H1])
        gap_exp = sb("gap_exp", [P, H1])
        den = sb("den", [P, H1])
        agg = sb("agg", [P, D])
        s_in = [sem(f"in{s}") for s in range(2)]
        s_gap = sem("gap")
        s_exp = sem("exp")
        s_dve = sem("dve")
        s_y = sem("y")
        s_st = [sem(f"stored{s}") for s in range(2)]
        block = ctx.enter_context(nc.Block())

        def over_tiles(eng, body):
            for t in range(2):
                body(t, t, t * P)
            with eng.Fori(1, TILES // 2) as i:
                for s in range(2):
                    body(2 * i + s, s, (2 * i + s) * P)
            body(TILES, TILES % 2, LAST0)

        def use(t, s):
            return t // 2 + 1 if isinstance(t, int) else (t - s) // 2 + 1

        @block.sync
        def _(sp):
            def load(t, s, r0):
                ge(sp, s_y, t - 1)
                sp.dma_start(x_in[s][:], x1[bass.ds(r0, P), :]).then_inc(s_in[s], 16)
                sp.dma_start(sums[s][:], acc[bass.ds(r0, P), :]).then_inc(s_in[s], 16)

            over_tiles(sp, load)

        @block.vector
        def _(dve):
            c = Chain(dve, s_dve)
            heads = lambda ap: ap.rearrange("p (h f) -> p h f", h=H1)

            def body(t, s, r0):
                c.start(3 * t)
                dve.wait_ge(s_in[s], 32 * use(t, s))
                nc.vector.tensor_tensor(gap[:], gmax[:], sums[s][:, D + H1:W], ALU.subtract).then_inc(s_gap, 1)
                dve.wait_ge(s_exp, t + 1)
                c.done(nc.vector.scalar_tensor_tensor(den[:], gap_exp[:], 1e-10, sums[s][:, D:D + H1], ALU.mult, ALU.add))
                c.after()
                c.done(nc.vector.reciprocal(den[:], den[:]))
                c.after()
                c.done(nc.vector.tensor_tensor(heads(agg[:]), heads(sums[s][:, 0:D]), bc(den[:], [P, H1, F1], 2), ALU.mult))
                c.after()
                ge(dve, s_st[s], 16 * (use(t, s) - 1))
                nc.vector.tensor_tensor(y[s][:], agg[:], x_in[s][:], ALU.add).then_inc(s_y, 1)

            over_tiles(dve, body)

        @block.scalar
        def _(act):
            def body(t, s, r0):
                act.wait_ge(s_gap, t + 1)
                ge(act, s_y, t)
                nc.scalar.activation(gap_exp[:], gap[:], ACT.Exp).then_inc(s_exp, 1)
                act.wait_ge(s_y, t + 1)
                if isinstance(t, int) and t == TILES:
                    act.wait_ge(s_st[1 - s], 16 * ((TILES + 1) // 2))
                act.dma_start(out[bass.ds(r0, P), :], y[s][:]).then_inc(s_st[s], 16)

            over_tiles(act, body)
            act.wait_ge(s_st[0], 16 * (TILES // 2 + 1))
            act.wait_ge(s_st[1], 16 * (TILES // 2))


def gnn_kernel(nc, x, src, dst, edge_attr_2, edge_attr_64, W_w, We_w, a_src, a_dst, a_edge, W_forward, W_reverse,
               attn_forward, out):
    table0 = nc.dram_tensor("table0", [N, W], F32).ap()
    table1 = nc.dram_tensor("table1", [N, W1], F32).ap()
    adst = nc.dram_tensor("adst", [NROWS, H0], F32).ap()
    acc0 = nc.dram_tensor("acc0", [NROWS, W], F32).ap()
    acc1 = nc.dram_tensor("acc1", [NROWS, W], F32).ap()
    x1 = nc.dram_tensor("x1", [N, D], F32).ap()
    dst_f = nc.dram_tensor("dst_f", [KSB * SB + J + 2], F32).ap()
    src_pad = nc.dram_tensor("src_pad", [KSB * SB], I32).ap()
    with ExitStack() as ctx:
        def sb(name, shape, dt=F32):
            return ctx.enter_context(nc.sbuf_tensor(name, shape, dt))

        keep = {
            "base_i": sb("base_i", [1, KSB], I32), "win_i": sb("win_i", [1, KSB + 1], I32),
            "base_f": sb("base_f", [P, KSB]), "last_rel": sb("last_rel_all", [P, KSB]),
            "minus_node": sb("minus_node_all", [P, KSB]), "edge_w": sb("edge_w", [P, 2 * H0]),
            "gmax_part": sb("gmax_part", [P, H1]),
        }
        gmax = sb("gmax", [P, H1])
        edge_tables(nc, src, dst, dst_f, src_pad, (acc0, acc1), adst, keep)
        node_stage(nc, 0, x, None, None, table0, adst,
                   {"W": W_w, "We": We_w, "a_src": a_src, "a_dst": a_dst, "a_edge": a_edge}, keep)
        edge_stage(nc, 0, table0, dst_f, src_pad, edge_attr_64, adst, acc0, keep, gmax)
        node_stage(nc, 1, x, acc0, x1, table1, None, {"Wf": W_forward, "Wr": W_reverse, "attn": attn_forward}, keep)
        edge_stage(nc, 1, table1, dst_f, src_pad, edge_attr_2, None, acc1, keep, gmax)
        final_stage(nc, x1, acc1, gmax, out)


_INS = ['x', 'src', 'dst', 'edge_attr_2', 'edge_attr_64', 'L0_gnn_W_w', 'L0_gnn_We_w', 'L0_gnn_a_src', 'L0_gnn_a_dst',
        'L0_gnn_a_edge', 'L1_gnn_W_forward', 'L1_gnn_W_reverse', 'L1_gnn_attn_forward']
_OUTS = [((6250, 256), 'float32')]


def kernel(**inputs):
    import numpy as _np
    import concourse.bacc as _bacc
    from concourse import mybir as _mybir
    from concourse.bass_utils import run_bass_kernel_spmd as _run

    nc = _bacc.Bacc("TRN2", target_bir_lowering=False, num_devices=1)
    arrays, args = {}, []
    for name in _INS:
        a = _np.ascontiguousarray(inputs[name])
        arrays[f"in_{name}_dram"] = a
        args.append(nc.dram_tensor(f"in_{name}_dram", a.shape, _mybir.dt.from_np(a.dtype), kind="ExternalInput").ap())
    for i, (shape, dtype) in enumerate(_OUTS):
        dt = _mybir.dt.from_np(_np.dtype(dtype))
        args.append(nc.dram_tensor(f"out_{i}_dram", shape, dt, kind="ExternalOutput").ap())
    gnn_kernel(nc, *args)
    r = _run(nc, [arrays], core_ids=[0])
    got = tuple(r.results[0][f"out_{i}_dram"] for i in range(len(_OUTS)))
    return got[0]
```

```python
from contextlib import ExitStack

import concourse.bass as bass
from concourse import mybir

F32 = mybir.dt.float32
I32 = mybir.dt.int32
BF16 = mybir.dt.bfloat16
ALU = mybir.AluOpType
ACT = mybir.ActivationFunctionType
AX_X = mybir.AxisListType.X

P = 128
N = 6250
E = 206250
D = 256
EF = 64
EPS = 1e-5
H0, F0 = 8, 32
H1, F1 = 4, 64

RING = 4
J = 14
SB = P * J
KSB = -(-E // SB)
KSB += -KSB % RING
FRONT = KSB * SB - E
assert 0 < FRONT < SB
W = D + 8
W1 = 2 * F1 + 2 * H1
WIN = 64
MAX_WINDOWS = KSB + N // WIN + 1
NROWS = 6400
TILES = N // P
LAST0 = N - P
BIG = 1.0e30
NO_NODE = -1.0


def ge(eng, sem, value):
    if not isinstance(value, int) or value > 0:
        eng.wait_ge(sem, value)


def bc(ap, shape, *axes):
    for a in axes:
        ap = ap.unsqueeze(a)
    return ap.to_broadcast(shape)


class Chain:

    def __init__(self, eng, sem):
        self.eng, self.sem, self.base, self.n = eng, sem, 0, 0

    def start(self, base):
        self.base, self.n = base, 0

    def done(self, ins):
        self.n += 1
        ins.then_inc(self.sem, 1)
        return self.n

    def after(self, n=None):
        ge(self.eng, self.sem, self.base + (self.n if n is None else n))


def bank(nc, ctx, name, shape):
    size = 1
    for n in shape[1:]:
        size *= n
    whole = ctx.enter_context(nc.psum_tensor(name, [P, -(-size // 512) * 512], F32))
    view = whole[0:shape[0], 0:size]
    if len(shape) == 2:
        return view
    axes = "abcd"[:len(shape) - 1]
    return view.rearrange(f"p ({' '.join(axes)}) -> p {' '.join(axes)}", **dict(zip(axes, shape[1:])))


def make_identity(nc, pool, ident, sem):
    nc.gpsimd.memset(ident[:], 0.0).then_inc(sem, 1)
    pool.wait_ge(sem, 1)
    nc.gpsimd.affine_select(out=ident[:], in_=ident[:], compare_op=ALU.not_equal, fill=1.0, base=0,
                            pattern=[[-1, P]], channel_multiplier=1).then_inc(sem, 1)


def edge_tables(nc, src, dst, dst_f, src_pad, acc, adst, keep):
    with ExitStack() as ctx:
        def sb(name, shape, dt=F32):
            return ctx.enter_context(nc.sbuf_tensor(name, shape, dt))

        def sem(name):
            return ctx.enter_context(nc.semaphore(name))

        R = 125
        edges = sb("et_edges", [R, E // R], I32)
        edges_f = sb("et_edges_f", [R, E // R])
        pad_f = sb("et_pad_f", [1, FRONT + 1])
        pad_i = sb("et_pad_i", [1, FRONT], I32)
        zero = sb("et_zero", [P, W])
        zero_bf = sb("et_zero_bf", [50, 9 * H0], BF16)
        ends_i = sb("et_ends_i", [1, 2 * KSB], I32)
        ends_f = sb("et_ends_f", [1, 2 * KSB])
        span_i = sb("et_span_i", [1, 2 * KSB], I32)
        span_f = sb("et_span_f", [1, 2 * KSB])
        ones = sb("et_ones", [1, KSB])
        ones_row = sb("et_ones_row", [1, P])
        rowid = sb("et_rowid", [P, 1])
        ends_ps = ctx.enter_context(nc.psum_tensor("et_ends_ps", [P, 2 * KSB], F32))
        s_dst = sem("et_dst")
        s_ends = sem("et_ends")
        s_set = sem("et_set")
        s_dve = sem("et_dve")
        s_pads = sem("et_pads")
        s_float = sem("et_float")
        s_bc = sem("et_bc")
        s_rowid = sem("et_rowid_sem")
        s_out = sem("et_out")
        block = ctx.enter_context(nc.Block())

        @block.sync
        def _(sp):
            sp.dma_start(edges[:], dst.rearrange("(p e) -> p e", p=R)).then_inc(s_dst, 16)
            sp.wait_ge(s_set, 1)
            with nc.allow_non_contiguous_dma(reason="one element per superblock"):
                body = dst[SB - FRONT:E]
                sp.dma_start(ends_i[:, 1:KSB], body.rearrange("(k e) -> k e", e=SB)[:, 0:1]
                             .rearrange("k e -> e k")).then_inc(s_ends, 16)
                sp.dma_start(ends_i[:, KSB + 1:2 * KSB], body.rearrange("(k e) -> k e", e=SB)[:, SB - 1:SB]
                             .rearrange("k e -> e k")).then_inc(s_ends, 16)
            sp.dma_start(ends_i[:, KSB:KSB + 1], dst[SB - FRONT - 1:SB - FRONT].unsqueeze(0)).then_inc(s_ends, 16)
            sp.dma_start(src_pad[FRONT:FRONT + E].rearrange("(p e) -> p e", p=R),
                         src.rearrange("(p e) -> p e", p=R)).then_inc(s_out, 16)
            sp.wait_ge(s_pads, 4)
            sp.dma_start(src_pad[0:FRONT].unsqueeze(0), pad_i[:]).then_inc(s_out, 16)
            sp.dma_start(dst_f[0:FRONT + 1].unsqueeze(0), pad_f[:]).then_inc(s_out, 16)
            sp.dma_start(dst_f[FRONT + 1 + E:FRONT + 1 + E + J + 1].unsqueeze(0), pad_f[:, 0:J + 1]).then_inc(s_out, 16)
            n_out = 4
            for a in acc:
                sp.dma_start(a.rearrange("(p r) c -> p r c", p=P),
                             bc(zero[:], [P, NROWS // P, W], 1)).then_inc(s_out, 16)
                n_out += 1
            sp.dma_start(adst[N:NROWS, :].rearrange("(p r) c -> p (r c)", p=50), zero_bf[0:50, :]).then_inc(s_out, 16)
            sp.wait_ge(s_float, 1)
            sp.dma_start(dst_f[FRONT + 1:FRONT + 1 + E].rearrange("(p e) -> p e", p=R), edges_f[:]).then_inc(s_out, 16)
            n_out += 2
            sp.wait_ge(s_out, 16 * n_out)

        @block.gpsimd
        def _(pool):
            nc.gpsimd.iota(rowid[:], pattern=[[0, 1]], base=0, channel_multiplier=1,
                           allow_small_or_imprecise_dtypes=True).then_inc(s_rowid, 1)

        @block.vector
        def _(dve):
            step = Chain(dve, s_dve)
            nc.vector.memset(ends_i[:], 0).then_inc(s_set, 1)
            nc.vector.memset(pad_f[:], NO_NODE).then_inc(s_pads, 1)
            nc.vector.memset(pad_i[:], 0).then_inc(s_pads, 1)
            nc.vector.memset(zero[:], 0.0).then_inc(s_pads, 1)
            nc.vector.memset(zero_bf[:], 0.0).then_inc(s_pads, 1)
            step.done(nc.vector.memset(ones[:], 1.0))
            step.done(nc.vector.memset(ones_row[:], 1.0))
            step.done(nc.vector.memset(keep["win_i"][:], 0))
            dve.wait_ge(s_dst, 16)
            nc.vector.tensor_copy(edges_f[:], edges[:]).then_inc(s_float, 1)
            dve.wait_ge(s_ends, 48)
            step.done(nc.vector.tensor_copy(keep["base_i"][:], ends_i[:, 0:KSB]))
            step.done(nc.vector.tensor_copy(ends_f[:], ends_i[:]))
            step.after()
            step.done(nc.vector.tensor_tensor(span_i[:, 0:KSB], ends_i[:, KSB:2 * KSB], ends_i[:, 0:KSB], ALU.subtract))
            step.after()
            step.done(nc.vector.tensor_single_scalar(span_i[:, KSB:2 * KSB], span_i[:, 0:KSB], WIN.bit_length() - 1, op=ALU.arith_shift_right))
            step.after()
            step.done(nc.vector.tensor_copy(span_f[:, 0:KSB], span_i[:, KSB:2 * KSB]))
            step.after()
            step.done(nc.vector.tensor_scalar(span_f[:, KSB:2 * KSB], span_f[:, 0:KSB], 1.0, None, ALU.add))
            step.after()
            step.done(nc.vector.tensor_tensor_scan(span_f[:, 0:KSB], ones[:], span_f[:, KSB:2 * KSB], 0.0,
                                                   ALU.mult, ALU.add))
            step.after()
            step.done(nc.vector.tensor_copy(keep["win_i"][:, 1:KSB + 1], span_f[:, 0:KSB]))
            dve.wait_ge(s_bc, 1)
            dve.wait_ge(s_rowid, 1)
            step.done(nc.vector.tensor_copy(keep["base_f"][:], ends_ps[:, 0:KSB]))
            step.after()
            step.done(nc.vector.tensor_tensor(keep["last_rel"][:], ends_ps[:, KSB:2 * KSB], keep["base_f"][:], ALU.subtract))
            step.done(nc.vector.tensor_scalar(keep["minus_node"][:], keep["base_f"][:], rowid[:, 0:1], -1.0,
                                              ALU.add, ALU.mult))
            step.after()

        @block.tensor
        def _(pe):
            pe.wait_ge(s_dve, 5)
            nc.tensor.matmul(ends_ps[:], ones_row[:], ends_f[:], start=True, stop=True).then_inc(s_bc, 1)


def over_tiles(eng, stages):
    lags = max(lag for lag, _ in stages)
    assert lags <= RING

    def step(u, s):
        for lag, fn in stages:
            t = u - lag
            if not isinstance(u, int):
                fn(t, (s - lag) % RING, t * P)
            elif 0 <= t <= TILES:
                fn(t, t % RING, t * P if t < TILES else LAST0)

    first, turns = RING, (TILES - RING) // RING
    for u in range(first):
        step(u, u)
    with eng.Fori(1, 1 + turns) as i:
        for s in range(RING):
            step(RING * i + s, s)
    for u in range(first + RING * turns, TILES + 1 + lags):
        step(u, u % RING)


def use_of(t, s):
    return t // RING + 1 if isinstance(t, int) else (t - s) // RING + 1


def node_stage(nc, layer, x, acc0, x1, table, adst, weights, keep):
    second = layer == 1
    cols = W + H0 if not second else W1
    width = W if not second else W1
    tag = f"n{layer}_"
    CH = TILES // 4
    with ExitStack() as ctx:
        def sb(name, shape, dt=F32):
            return ctx.enter_context(nc.sbuf_tensor(tag + name, shape, dt))

        def sem(name):
            return ctx.enter_context(nc.semaphore(tag + name))

        def ps(name, shape):
            return bank(nc, ctx, tag + name, shape)

        ident = sb("ident", [P, P])
        rhs = sb("rhs", [P, 2, cols])
        xs = sb("xs", [P, TILES + 1, D])
        stats = [sb(f"stats{b}", [P, nc.vector.BN_STATS_DIM]) for b in range(2)]
        mv = [sb(f"mv{b}", [P, nc.vector.BN_AGGR_DIM]) for b in range(2)]
        mean = sb("mean", [P, TILES + 1])
        var_eps = sb("var_eps", [P, TILES + 1])
        std = sb("std", [P, TILES + 1])
        rstd = sb("rstd", [P, TILES + 1])
        h = [sb(f"h{s}", [P, D]) for s in range(RING)]
        hT = [sb(f"hT{s}", [P, 2, P]) for s in range(RING)]
        row = [sb(f"row{s}", [P, cols]) for s in range(RING)]
        hT_ps = [ps(f"hT_ps{b}", [P, 2, P]) for b in range(2)]
        row_ps = [ps(f"row_ps{b}", [P, cols]) for b in range(2)]
        w_ps = ps("w_ps", [P, 512])
        if not second:
            w_in = sb("w_in", [P, 2, D])
            a_row = sb("a_row", [P, 3, D])
            we = sb("we", [P, D])
            prod = sb("prod", [P, D])
            parts = [sb(f"parts{s}", [P, 3 * H0], BF16) for s in range(RING)]
            rest = sb("rest", [P, 2 * H0])
        else:
            w_in = sb("w_in", [F1, 2, D])
            a_row = sb("a_row", [F1, H1])
            sums = [sb(f"sums{s}", [P, W]) for s in range(RING)]
            den = sb("den", [P, 2 * H0])
            agg = [sb(f"agg{s}", [P, D]) for s in range(RING)]
            low = [sb(f"low{s}", [P, D]) for s in range(RING)]
            low_exp = [sb(f"low_exp{s}", [P, D]) for s in range(RING)]
            part_new = sb("part_new", [P, D])

        s_id = sem("id")
        s_w = sem("w")
        s_wdve = sem("wdve")
        s_rhs = sem("rhs_ready")
        s_x = [sem(f"x_in{n}") for n in range(5)]
        s_gate = sem("gate")
        s_stat = sem("stat_steps")
        s_var = sem("var_ready")
        s_std = sem("std_ready")
        s_rstd = sem("rstd_ready")
        s_h = sem("h_ready")
        s_hTp = sem("hT_turned")
        s_hT = sem("hT_ready")
        s_rowp = sem("row_summed")
        s_row = sem("row_ready")
        s_st = [sem(f"stored{s}") for s in range(RING)]
        if not second:
            s_split = sem("split_steps")
            s_parts = sem("parts_ready")
        else:
            s_wps = sem("wps")
            s_sums = [sem(f"sums_in{s}") for s in range(RING)]
            s_agg = sem("agg_steps")
            s_low = sem("low_ready")
            s_exp = sem("exp_ready")
            s_upd = sem("update_steps")
            s_new = sem("x_new_ready")
            s_x1 = sem("x1_stored")
        block = ctx.enter_context(nc.Block())
        STORES = 1 if second else 2

        def tiles_of(a, n):
            return a[n * CH * P:(n + 1) * CH * P, :].rearrange("(t p) c -> p t c", p=P)

        @block.sync
        def _(sp):
            for n in range(4):
                sp.dma_start(xs[:, n * CH:(n + 1) * CH, :], tiles_of(x, n)).then_inc(s_x[n], 16)
            sp.dma_start(xs[:, TILES, :], x[LAST0:N, :]).then_inc(s_x[4], 16)
            if not second:
                sp.dma_start(w_in[:], weights["W"].rearrange("(c p) n -> p c n", p=P)).then_inc(s_w, 16)
                for n, a in enumerate(("a_src", "a_dst", "a_edge")):
                    sp.dma_start(a_row[:, n, :], bc(weights[a].rearrange("h f -> (h f)"), [P, D], 0)).then_inc(s_w, 16)
                for half in range(2):
                    sp.dma_start(we[EF * half:EF * half + EF, :], weights["We"]).then_inc(s_w, 16)
            else:
                sp.dma_start(w_in[:, 0, :], weights["Wf"]).then_inc(s_w, 16)
                sp.dma_start(w_in[:, 1, :], weights["Wr"]).then_inc(s_w, 16)
                with nc.allow_non_contiguous_dma(reason="256 weights, turned"):
                    sp.dma_start(a_row[:], weights["attn"][0].rearrange("h f -> f h")).then_inc(s_w, 16)

                def load(t, s, r0):
                    ge(sp, s_low, t - RING + 1)
                    sp.dma_start(sums[s][:], acc0[bass.ds(r0, P), :]).then_inc(s_sums[s], 16)

                over_tiles(sp, [(0, load)])
                sp.wait_ge(s_new, TILES + 1)
                for n in range(4):
                    sp.dma_start(tiles_of(x1, n), xs[:, n * CH:(n + 1) * CH, :]).then_inc(s_x1, 16)
                sp.wait_ge(s_x1, 64)
                sp.dma_start(x1[LAST0:N, :], xs[:, TILES, :]).then_inc(s_x1, 16)
                sp.wait_ge(s_x1, 80)

        @block.gpsimd
        def _(pool):
            make_identity(nc, pool, ident, s_id)

        @block.vector
        def _(dve):
            V = nc.vector
            stat_c = Chain(dve, s_stat)

            def statistics(t, s):
                c, b, xt = stat_c, s % 2, xs[:, bass.ds(t, 1), :].rearrange("p o d -> p (o d)")
                c.start(3 * t)
                c.done(V.bn_stats(stats[b][:], xt))
                c.after()
                dve.sem_inc(s_gate, 1)
                c.done(V.bn_aggr(mv[b][:], stats[b][:]))
                c.after()
                c.done(V.tensor_copy(mean[:, bass.ds(t, 1)], mv[b][:, 0:1]))
                V.tensor_scalar(var_eps[:, bass.ds(t, 1)], mv[b][:, 1:2], EPS, None, ALU.add).then_inc(s_var, 1)

            if not second:
                for n in range(4):
                    dve.wait_ge(s_x[n], 16)
                    with dve.Fori(n * CH // 2, (n + 1) * CH // 2) as i:
                        for b in range(2):
                            statistics(2 * i + b, b)
                dve.wait_ge(s_x[4], 16)
                statistics(TILES, 0)
            else:
                agg_c, upd_c = Chain(dve, s_agg), Chain(dve, s_upd)
                heads = lambda ap: ap.rearrange("p (h f) -> p h f", h=H0)

                def divide(t, s, r0):
                    c = agg_c
                    c.start(3 * t)
                    dve.wait_ge(s_sums[s], 16 * use_of(t, s))
                    c.done(V.tensor_scalar(den[:, 0:H0], sums[s][:, D:D + H0], 1e-30, None, ALU.max))
                    c.after()
                    c.done(V.reciprocal(den[:, H0:2 * H0], den[:, 0:H0]))
                    c.after()
                    c.done(V.tensor_tensor(heads(agg[s][:]), heads(sums[s][:, 0:D]),
                                           bc(den[:, H0:2 * H0], [P, H0, F0], 2), ALU.mult))
                    c.after()
                    V.tensor_scalar(low[s][:], agg[s][:], 0.0, None, ALU.min).then_inc(s_low, 1)

                def update(t, s, r0):
                    c, xt = upd_c, xs[:, bass.ds(t, 1), :].rearrange("p o d -> p (o d)")
                    c.start(t)
                    c.done(V.scalar_tensor_tensor(part_new[:], agg[s][:], 0.0, xt, ALU.max, ALU.add))
                    dve.wait_ge(s_exp, t + 1)
                    c.after()
                    V.scalar_tensor_tensor(xt, low_exp[s][:], -1.0, part_new[:], ALU.add, ALU.add).then_inc(s_new, 1)
                    dve.wait_ge(s_new, t + 1)
                    dve.sem_inc(s_gate, 1)
                    statistics(t, s)

                for n in range(5):
                    dve.wait_ge(s_x[n], 16)
                over_tiles(dve, [(0, divide), (1, update)])
            dve.wait_ge(s_std, 1)
            V.reciprocal(rstd[:], std[:]).then_inc(s_rstd, 1)

            step = Chain(dve, s_wdve)
            if not second:
                dve.wait_ge(s_w, 96)
                step.done(V.memset(keep["edge_w"][:], 0.0))
                for c in range(2):
                    V.tensor_copy(rhs[:, c, 0:D], w_in[:, c, :]).then_inc(s_rhs, 1)
                    for n in range(2):
                        step.after()
                        step.done(V.tensor_tensor(prod[:], w_in[:, c, :], a_row[:, n, :], ALU.mult))
                        step.after()
                        step.done(V.tensor_reduce(rhs[:, c, D + n * H0:D + (n + 1) * H0],
                                                  prod[:].rearrange("p (h f) -> p h f", h=H0), AX_X, ALU.add))
                step.after()
                step.done(V.tensor_tensor(prod[:], we[:], a_row[:, 2, :], ALU.mult))
                step.after()
                for half in range(2):
                    q = slice(EF * half, EF * half + EF)
                    step.done(V.tensor_reduce(keep["edge_w"][q, H0 * half:H0 * half + H0],
                                              prod[q, :].rearrange("p (h f) -> p h f", h=H0), AX_X, ALU.add))
                step.after()
                dve.sem_inc(s_rhs, 1)
            else:
                dve.wait_ge(s_wps, 2)
                V.tensor_copy(rhs[:].rearrange("p c n -> p (c n)"), w_ps[:, 0:2 * W1]).then_inc(s_rhs, 3)
            dve.wait_ge(s_rstd, 1)

            def normalize(t, s, r0):
                ge(dve, s_hTp, t - RING + 1)
                V.tensor_scalar(h[s][:], xs[:, bass.ds(t, 1), :].rearrange("p o d -> p (o d)"), mean[:, bass.ds(t, 1)],
                                rstd[:, bass.ds(t, 1)], ALU.subtract, ALU.mult).then_inc(s_h, 1)

            def split_adst(t, s, r0):
                c = Chain(dve, s_split)
                c.start(4 * t)
                dve.wait_ge(s_row, t + 1)
                ge(dve, s_st[s], 16 * STORES * (use_of(t, s) - 1))
                a = row[s][:, W:W + H0]
                part = lambda n: parts[s][:, n * H0:(n + 1) * H0]
                c.done(V.tensor_copy(part(0), a))
                c.after()
                c.done(V.tensor_tensor(rest[:, 0:H0], a, part(0), ALU.subtract))
                c.after()
                c.done(V.tensor_copy(part(1), rest[:, 0:H0]))
                c.after()
                c.done(V.tensor_tensor(rest[:, H0:2 * H0], rest[:, 0:H0], part(1), ALU.subtract))
                c.after()
                V.tensor_copy(part(2), rest[:, H0:2 * H0]).then_inc(s_parts, 1)

            over_tiles(dve, [(0, normalize)] + ([] if second else [(3, split_adst)]))

        @block.tensor
        def _(pe):
            pe.wait_ge(s_id, 2)
            if second:
                pe.wait_ge(s_w, 48)
                for c in range(2):
                    cs = slice(c * P, (c + 1) * P)
                    o = c * W1
                    for n in range(2):
                        nc.tensor.transpose(w_ps[:, o + n * F1:o + (n + 1) * F1], w_in[:, n, cs], ident[0:F1, 0:F1])
                        last = nc.tensor.matmul(w_ps[:, o + 2 * F1 + n * H1:o + 2 * F1 + (n + 1) * H1],
                                                w_in[:, n, cs], a_row[:], start=True, stop=True)
                    last.then_inc(s_wps, 1)
            pe.wait_ge(s_rhs, 3)

            def turn(t, s, r0):
                pe.wait_ge(s_h, t + 1)
                ge(pe, s_hT, t - 1)
                for c in range(2):
                    last = nc.tensor.transpose(hT_ps[s % 2][:, c, :], h[s][:, c * P:(c + 1) * P], ident[:])
                last.then_inc(s_hTp, 1)

            def product(t, s, r0):
                pe.wait_ge(s_hT, t + 1)
                ge(pe, s_row, t - 1)
                for c in range(2):
                    last = nc.tensor.matmul(row_ps[s % 2], hT[s][:, c, :], rhs[:, c, :], start=(c == 0), stop=(c == 1))
                last.then_inc(s_rowp, 1)

            over_tiles(pe, [(0, turn), (1, product)])

        @block.scalar
        def _(act):
            if second:
                def low_exps(t, s, r0):
                    act.wait_ge(s_low, t + 1)
                    ge(act, s_new, t - RING + 1)
                    nc.scalar.activation(low_exp[s][:], low[s][:], ACT.Exp).then_inc(s_exp, 1)

                over_tiles(act, [(0, low_exps)])
            act.wait_ge(s_var, TILES + 1)
            nc.scalar.activation(std[:], var_eps[:], ACT.Sqrt).then_inc(s_std, 1)

            def relu(t, s, r0):
                act.wait_ge(s_hTp, t + 1)
                ge(act, s_rowp, t - RING + 1)
                nc.scalar.activation(hT[s][:], hT_ps[s % 2], ACT.Relu).then_inc(s_hT, 1)

            def copy_row(t, s, r0):
                act.wait_ge(s_rowp, t + 1)
                ge(act, s_st[s], 16 * STORES * (use_of(t, s) - 1))
                nc.scalar.copy(row[s][:], row_ps[s % 2]).then_inc(s_row, 1)

            def store(t, s, r0):
                if isinstance(t, int) and t == TILES:
                    act.wait_ge(s_st[(TILES - 1) % RING], 16 * STORES * use_of(TILES - 1, (TILES - 1) % RING))
                act.wait_ge(s_row, t + 1)
                act.dma_start(table[bass.ds(r0, P), :], row[s][:, 0:width]).then_inc(s_st[s], 16)
                if not second:
                    act.wait_ge(s_parts, t + 1)
                    act.dma_start(adst[bass.ds(r0, P), :], parts[s][:]).then_inc(s_st[s], 16)

            over_tiles(act, [(0, relu), (1, copy_row), (3, store)])
            for s in range(RING):
                act.wait_ge(s_st[s], 16 * STORES * (-(-(TILES + 1 - s) // RING)))


def edge_stage(nc, layer, table, dst_f, src_pad, attr, adst, acc, keep, gmax, rings):
    first_layer = layer == 0
    H = H0 if first_layer else H1
    TW = W if first_layer else W1
    HJ = H * J
    AF = EF if first_layer else 2
    tag = f"e{layer}_"
    with ExitStack() as ctx:
        def sb(name, shape, dt=F32):
            return ctx.enter_context(nc.sbuf_tensor(tag + name, shape, dt))

        def sem(name):
            return ctx.enter_context(nc.semaphore(tag + name))

        def ps(name, shape):
            return bank(nc, ctx, tag + name, shape)

        ident = sb("ident", [P, P])
        iota = sb("iota", [P, WIN])
        rowid = sb("rowid", [P, 1])
        zero_row = sb("zero_row", [1, 512], BF16)
        idx = [sb(f"idx{s}", [P, J], I32) for s in range(RING)]
        dwin = [sb(f"dwin{s}", [P, J + 2]) for s in range(RING)]
        att = [sb(f"att{s}", [P, J, AF]) for s in range(RING)]
        rows = [sb(f"rows{s}", [P, J, TW]) for s in range(RING)]
        drel = [sb(f"drel{b}", [P, J + 1]) for b in range(2)]
        last_rel = [sb(f"last_rel{b}", [P, 1]) for b in range(2)]
        headmask = sb("headmask", [P, J])
        tailmask = sb("tailmask", [P, J])
        cut = sb("cut", [P, J + 1])
        link = sb("link", [P, HJ + 1])
        score = sb("score", [P, H, J])
        fwd = sb("fwd", [P, H, J])
        bwd = sb("bwd", [P, H, J])
        edge_links = sb("edge_links", [P, 2, H])
        links_T = sb("links_T", [H, 2, P])
        fwd_T = sb("fwd_T", [H, P + 1])
        bwd_T = sb("bwd_T", [H, P + 1])
        local = sb("local", [P, H, J])
        from_prev = sb("from_prev", [P, H, J])
        from_next = sb("from_next", [P, H, J])
        across = sb("across", [P, H, J])
        top = sb("top", [P, H, J])
        z = sb("z", [P, H, J])
        z_old = sb("z_old", [P, H])
        fade = sb("fade", [P, H])
        msg = [sb(f"msg{b}", [P, J, W]) for b in range(2)]
        onehot = sb("onehot", [P, J, WIN])
        onehot_carry = sb("onehot_carry", [1, WIN])
        pick_last = sb("pick_last", [WIN, 1])
        carry = sb("carry", [1, W])
        out_rows = sb("out_rows", [WIN, W])

        sums_ps = ps("sums_ps", [WIN, W])
        ends_ps = ps("ends_ps", [H, 4, P])
        back_ps = ps("back_ps", [P, 2, H])
        carry_ps = ps("carry_ps", [1, W])
        if first_layer:
            old = sb("old", [P, H])
            both = sb("both", [P, 2, H, J])
            both_l = sb("both_l", [P, 2, H, J])
            old_l = sb("old_l", [P, H])
            att_T = sb("att_T", [P, J // 2, P])
            dst_bc = [sb(f"dst_bc{b}", [WIN, SB]) for b in range(2)]
            dist = sb("dist", [WIN, SB])
            node_hot = sb("node_hot", [WIN, SB], BF16)
            minus_node = sb("minus_node", [WIN, 1])
            adst_win = sb("adst_win", [WIN, 3 * H0], BF16)
            att_ps = ps("att_ps", [P, J // 2, P])
            ae_ps = ps("ae_ps", [P, J, H0])
            ad_ps = ps("ad_ps", [P, J, 3 * H0])
            edge_w = keep["edge_w"]
            edge_score = [sb(f"edge_score{b}", [P, J, H0]) for b in range(2)]
            node_parts = [sb(f"node_parts{b}", [P, J, 3 * H0]) for b in range(2)]
            node_two = sb("node_two", [P, H, J])
            node_score = sb("node_score", [P, H, J])
        else:
            t0 = sb("t0", [P, H, J])
            t1 = sb("t1", [P, H, J])
            t2 = sb("t2", [P, H, J])
            kmax = sb("kmax", [P, H])
            fwd_msg = [sb(f"fwd_msg{b}", [P, J, F1]) for b in range(2)]
            rev_msg = [sb(f"rev_msg{b}", [P, J, F1]) for b in range(2)]
            mix = sb("mix", [P, J, F1])

        s_setup = sem("setup")
        s_dve_setup = sem("dve_setup")
        s_pool_setup = sem("pool_setup")
        s_idx, s_dwin, s_att, s_rows = rings
        s_go = sem("slot_granted")
        s_gate = sem("gate")
        s_att_used = sem("att_used")
        s_scan = sem("scan_steps")
        s_max = sem("max_steps")
        s_prod = sem("product_steps")
        s_links_T = sem("links_T_ready")
        s_ends = sem("ends_turned")
        s_T = sem("scans_T_ready")
        s_back = sem("back_turned")
        s_z = sem("z_ready")
        s_exp = sem("exp_ready")
        s_msg = sem("msg_ready")
        s_fresh = sem("carry_ready")
        s_hot = sem("onehot_ready")
        s_mm = sem("window_summed")
        s_out = sem("out_rows_ready")
        s_carry = sem("carry_picked")
        s_stored = sem("stored")
        s_out_free = sem("out_rows_stored")
        if first_layer:
            s_dstbc = [sem(f"dst_bc_in{b}") for b in range(2)]
            s_adw = sem("adst_win_in")
            s_dstbc_used = sem("dst_bc_used")
            s_act = sem("act")
            s_node_hot = sem("node_hot_ready")
            s_spread = sem("adst_spread")
            s_ad = sem("ad_ready")
            s_attp = sem("att_turned")
            s_attT = sem("att_T_ready")
            s_ae = sem("ae_ready")
            s_edge_score = sem("edge_score_ready")
            s_node_score = sem("node_parts_ready")
        else:
            s_mix = sem("fwd_rev_ready")
        block = ctx.enter_context(nc.Block())
        SCAN = 11 if first_layer else 17
        MAX = 13 if first_layer else 6
        PROD = 1
        FRESH = 2 if first_layer else 3

        def over_superblocks(eng, body):
            for s in range(RING):
                body(s, s, RING)
            with eng.Fori(1, KSB // RING - 1) as i:
                for s in range(RING):
                    body(RING * i + s, s, RING)
            for s in range(RING):
                body(KSB - RING + s, s, RING - 1 - s)

        def use(k, s, ring):
            before = 0 if first_layer else KSB // ring
            return before + (k // ring + 1 if isinstance(k, int) else (k - s) // ring + 1)

        def window_bounds(eng, k):
            lo = eng.value_load(keep["win_i"][0:1, bass.ds(k, 1)], min_val=0, max_val=MAX_WINDOWS)
            hi = eng.value_load(keep["win_i"][0:1, bass.ds(k + 1, 1)], min_val=1, max_val=MAX_WINDOWS)
            return lo, hi

        def window_row(eng, base, w, lo):
            return nc.s_assert_within(eng.snap(base + (w - lo) * WIN), 0, NROWS - WIN, skip_runtime_bounds_check_because=
                                      "a window begins at or before its superblock's last destination")

        @block.sync
        def _(sp):
            def load(k, s):
                n = use(k, s, RING)
                e0 = SB * k
                ge(sp, s_rows[s], 16 * J * (n - 1))
                sp.dma_start(idx[s][:], src_pad[bass.ds(e0, SB)].rearrange("(p j) -> p j", p=P)).then_inc(s_idx[s], 16)
                ge(sp, s_scan, (k - RING + 1) * SCAN)
                sp.dma_start(dwin[s][:, 0:J], dst_f[bass.ds(e0, SB)].rearrange("(p j) -> p j", p=P))\
                  .then_inc(s_dwin[s], 16)
                sp.dma_start(dwin[s][:, J:J + 2], dst_f[bass.ds(e0 + J, SB)].rearrange("(p j) -> p j", p=P)[:, 0:2])\
                  .then_inc(s_dwin[s], 16)
                ge(sp, s_att_used, k - RING + 1)
                if isinstance(k, int) and k == 0:
                    p0, j0 = FRONT // J, FRONT % J
                    part = J - j0
                    sp.wait_ge(s_setup, 1)
                    sp.dma_start(att[s][p0:p0 + 1, j0:J, :], attr[0:part, :].unsqueeze(0)).then_inc(s_att[s], 16)
                    sp.dma_start(att[s][p0 + 1:P, :, :], attr[part:SB - FRONT, :].rearrange("(p j) c -> p j c", j=J))\
                      .then_inc(s_att[s], 16)
                else:
                    sp.dma_start(att[s][:], attr[bass.ds(e0 - FRONT, SB), :].rearrange("(p j) c -> p j c", j=J))\
                      .then_inc(s_att[s], 16)

            def load_dst_bc(k, b):
                ge(sp, s_dstbc_used, k - 1)
                sp.dma_start(dst_bc[b][:], bc(dst_f[bass.ds(SB * k + 1, SB)], [WIN, SB], 0)).then_inc(s_dstbc[b], 16)

            def load_adst(k):
                base = sp.value_load(keep["base_i"][0:1, bass.ds(k, 1)], min_val=0, max_val=N - 1)
                lo, hi = window_bounds(sp, k)
                with sp.Fori(lo, hi) as w:
                    sp.wait_ge(s_spread, w + 1)
                    sp.dma_start(adst_win[:], adst[bass.ds(window_row(sp, base, w, lo), WIN), :]).then_inc(s_adw, 16)

            if first_layer:
                sp.sem_inc(s_spread, 1)
            sp.sem_inc(s_out_free, 1)
            for s in range(RING):
                load(s, s)
            if first_layer:
                for k in range(RING):
                    load_dst_bc(k, k % 2)
                    if k < RING - 1:
                        load_adst(k)

            def body(k, s, left):
                if left == RING:
                    load(k + RING, s)
                    if first_layer:
                        load_dst_bc(k + RING, s % 2)
                if first_layer and left >= RING - 1:
                    load_adst(k + RING - 1)
                base = sp.value_load(keep["base_i"][0:1, bass.ds(k, 1)], min_val=0, max_val=N - 1)
                lo, hi = window_bounds(sp, k)
                with sp.Fori(lo, hi) as w:
                    sp.wait_ge(s_out, w + 1)
                    sp.dma_start(acc[bass.ds(window_row(sp, base, w, lo), WIN), :], out_rows[:]).then_inc(s_stored, 16)
                    sp.wait_ge(s_stored, 16 * w + 16)
                    sp.sem_inc(s_out_free, 1)

            over_superblocks(sp, body)

        @block.gpsimd
        def _(pool):
            make_identity(nc, pool, ident, s_pool_setup)
            nc.gpsimd.iota(iota[:], pattern=[[1, WIN]], base=0, channel_multiplier=0,
                           allow_small_or_imprecise_dtypes=True).then_inc(s_pool_setup, 1)
            nc.gpsimd.iota(rowid[:], pattern=[[0, 1]], base=0, channel_multiplier=1,
                           allow_small_or_imprecise_dtypes=True).then_inc(s_pool_setup, 1)

            def body(k, s, left):
                pool.wait_ge(s_idx[s], 16 * use(k, s, RING))
                ge(pool, s_msg, k - RING + 1)
                pool.sem_inc(s_go, 1)
                for j in range(J):
                    pool.indirect_dma_start(rows[s][:, j, :], None, table[:, :],
                                            bass.IndirectOffsetOnAxis(ap=idx[s][:, j:j + 1], axis=0))\
                        .then_inc(s_rows[s], 16)

            over_superblocks(pool, body)
            if not first_layer:
                pool.wait_ge(s_scan, KSB * SCAN)
                nc.gpsimd.partition_all_reduce(gmax[:], keep["gmax_part"][:], P, bass.bass_isa.ReduceOp.max)\
                    .then_inc(s_go, 1)
                pool.wait_ge(s_go, KSB + 1)

        @block.vector
        def _(dve):
            V = nc.vector
            V.memset(link[:], -BIG).then_inc(s_dve_setup, 1)
            V.memset(fwd_T[:], -BIG).then_inc(s_dve_setup, 1)
            V.memset(bwd_T[:], -BIG).then_inc(s_dve_setup, 1)
            V.memset(zero_row[:], 0.0).then_inc(s_dve_setup, 1)
            V.memset(att[0][:], 0.0).then_inc(s_setup, 1)
            dve.wait_ge(s_dve_setup, 4)
            dve.wait_ge(s_pool_setup, 4)
            scan, high, prod = Chain(dve, s_scan), Chain(dve, s_max), Chain(dve, s_prod)
            hj = [P, H, J]
            flat = lambda t: t[:].rearrange("p h j -> p (h j)")

            def scores_and_scans(k, s):
                n, b, c = use(k, s, RING), s % 2, scan
                c.start(k * SCAN)
                dw = dwin[s]
                dve.wait_ge(s_dwin[s], 32 * n)
                if not first_layer:
                    ge(dve, s_fresh, FRESH * (k - 1) + 1)
                c.done(V.tensor_scalar(drel[b][:], dw[:, 0:J + 1], keep["base_f"][:, bass.ds(k, 1)], None, ALU.subtract))
                c.done(V.tensor_copy(last_rel[b][:], keep["last_rel"][:, bass.ds(k, 1)]))
                c.done(V.tensor_scalar(headmask[:], dw[:, 1:J + 1], dw[:, 0:1], -BIG, ALU.not_equal, ALU.mult))
                c.done(V.tensor_scalar(tailmask[:], dw[:, 1:J + 1], dw[:, J + 1:J + 2], -BIG, ALU.not_equal, ALU.mult))
                c.done(V.tensor_tensor(cut[:], dw[:, 1:J + 2], dw[:, 0:J + 1], ALU.not_equal))
                c.after()
                c.done(V.tensor_scalar(link[:, 0:HJ].rearrange("p (h j) -> p h j", h=H)[:, :, 1:J],
                                       bc(cut[:, 1:J], [P, H, J - 1], 1), -BIG, None, ALU.mult))
                c.done(V.tensor_copy(edge_links[:, 0, :], headmask[:, J - 1:J].to_broadcast([P, H])))
                c.done(V.tensor_copy(edge_links[:, 1, :], tailmask[:, 0:1].to_broadcast([P, H])))
                dve.wait_ge(s_rows[s], 16 * J * n)
                if first_layer:
                    dve.wait_ge(s_edge_score, k + 1)
                    c.done(V.tensor_tensor(score[:], rows[s][:, :, D:D + H].rearrange("p j h -> p h j"),
                                           edge_score[b][:].rearrange("p j h -> p h j"), ALU.add))
                else:
                    dve.wait_ge(s_att[s], att_landed(k, s))
                    up = rows[s][:, :, 2 * F1:2 * F1 + 2 * H1].rearrange("p j (d h) -> p d h j", d=2)
                    c.done(V.tensor_tensor(t0[:], up[:, 0], bc(att[s][:, :, 0], hj, 1), ALU.mult))
                    c.done(V.tensor_tensor(t1[:], up[:, 1], bc(att[s][:, :, 1], hj, 1), ALU.mult))
                    c.after()
                    c.done(V.tensor_tensor(t2[:], t0[:], t1[:], ALU.add))
                    c.after()
                    c.done(V.scalar_tensor_tensor(score[:], t2[:], 0.2, t2[:], ALU.mult, ALU.max))
                c.after()
                if not first_layer:
                    if isinstance(k, int) and k == 0:
                        c.done(V.tensor_scalar(t0[:, 0, :], dw[:, 1:J + 1], NO_NODE, -BIG, ALU.is_equal, ALU.mult))
                        c.after()
                        c.done(V.tensor_tensor(t1[:], score[:], bc(t0[:, 0, :], hj, 1), ALU.add))
                        c.after()
                        c.done(V.tensor_reduce(keep["gmax_part"][:], t1[:], AX_X, ALU.max))
                    else:
                        c.done(V.tensor_reduce(kmax[:], score[:], AX_X, ALU.max))
                        c.after()
                        c.done(V.tensor_tensor(keep["gmax_part"][:], keep["gmax_part"][:], kmax[:], ALU.max))
                        c.done(V.memset(t0[:, 0, 0:1], 0.0))
                c.done(V.tensor_tensor_scan(flat(fwd), link[:, 0:HJ], flat(score), -BIG, ALU.add, ALU.max))
                c.done(V.tensor_tensor_scan(flat(bwd)[:, ::-1], link[:, 1:HJ + 1][:, ::-1], flat(score)[:, ::-1],
                                            -BIG, ALU.add, ALU.max))
                assert c.n == SCAN, (layer, c.n)

            def att_landed(k, s):
                return 16 * use(k, s, RING) + (16 * (layer + 1) if s == 0 else 0)

            def scans_across(k, s):
                c = high
                c.start(k * MAX)
                c.done(V.tensor_copy(fwd_T[:, 0:1], fwd_T[:, P:P + 1]))
                scan.start(k * SCAN)
                scan.after(SCAN)
                c.done(V.tensor_tensor(local[:], fwd[:], bwd[:], ALU.max))
                c.after(1)
                dve.wait_ge(s_links_T, k + 1)
                V.tensor_tensor_scan(fwd_T[:, 1:P + 1], links_T[:, 0, :], ends_ps[:, 0, :], fwd_T[:, 0:1],
                                     ALU.add, ALU.max).then_inc(s_T, 1)
                V.tensor_tensor_scan(bwd_T[:, 0:P][:, ::-1], links_T[:, 1, :][:, ::-1], ends_ps[:, 1, :][:, ::-1],
                                     -BIG, ALU.add, ALU.max).then_inc(s_T, 1)

            def maxima(k, s, lo_before):
                b, c = s % 2, high
                c.start(k * MAX)
                c.n = 2
                if first_layer:
                    dve.wait_ge(s_node_score, k + 1)
                    part = lambda q: node_parts[b][:, :, q * H:(q + 1) * H].rearrange("p j h -> p h j")
                    c.done(V.tensor_tensor(node_two[:], part(0), part(1), ALU.add))
                dve.wait_ge(s_back, k + 1)
                c.done(V.tensor_tensor(from_prev[:], bc(headmask[:], hj, 1), bc(back_ps[:, 0, :], hj, 2), ALU.add))
                c.done(V.tensor_tensor(from_next[:], bc(tailmask[:], hj, 1), bc(back_ps[:, 1, :], hj, 2), ALU.add))
                if first_layer:
                    c.after(3)
                    c.done(V.tensor_tensor(node_score[:], node_two[:], part(2), ALU.add))
                    c.after(5)
                    c.done(V.tensor_tensor(across[:], from_prev[:], from_next[:], ALU.max))
                    c.after(6)
                    c.done(V.tensor_tensor(both[:, 0], score[:], node_score[:], ALU.add))
                    c.done(V.tensor_tensor(old[:], from_prev[:, :, 0], node_score[:, :, 0], ALU.add))
                    c.after(7)
                    c.done(V.tensor_tensor(top[:], across[:], local[:], ALU.max))
                    c.after(9)
                    c.done(V.scalar_tensor_tensor(old_l[:], old[:], 0.01, old[:], ALU.mult, ALU.max))
                    c.after(10)
                    c.done(V.tensor_tensor(both[:, 1], top[:], node_score[:], ALU.add))
                    c.after()
                    c.done(V.scalar_tensor_tensor(both_l[:], both[:], 0.01, both[:], ALU.mult, ALU.max))
                    c.after()
                    score_l, top_l, old_v = both_l[:, 0], both_l[:, 1], old_l[:]
                else:
                    c.after()
                    c.done(V.tensor_tensor(across[:], from_prev[:], from_next[:], ALU.max))
                    c.after()
                    c.done(V.tensor_tensor(top[:], across[:], local[:], ALU.max))
                    c.after()
                    score_l, top_l, old_v = score[:], top[:], from_prev[:, :, 0]
                assert c.n == MAX, (layer, c.n)
                ge(dve, s_exp, 2 * k)
                V.tensor_tensor(z[:], score_l, top_l, ALU.subtract).then_inc(s_z, 1)
                V.tensor_tensor(z_old[:], old_v, top_l[:, :, 0], ALU.subtract).then_inc(s_z, 1)

            def products(k, s):
                b = s % 2
                m = msg[b]
                dve.wait_ge(s_exp, 2 * k + 2)
                heads = m[:, :, 0:D].rearrange("p j (h f) -> p j h f", h=H)
                if first_layer:
                    V.tensor_tensor(heads, rows[s][:, :, 0:D].rearrange("p j (h f) -> p j h f", h=H),
                                    bc(m[:, :, D:D + H], [P, J, H, F0], 3), ALU.mult).then_inc(s_msg, 1)
                else:
                    prod.start(k * PROD)
                    dve.wait_ge(s_mix, 2 * J * k + 2 * J)
                    prod.done(V.tensor_tensor(mix[:], fwd_msg[b][:], rev_msg[b][:], ALU.add))
                    prod.after()
                    V.tensor_tensor(heads, bc(mix[:], [P, J, H, F1], 2), bc(m[:, :, D:D + H], [P, J, H, F1], 3),
                                    ALU.mult).then_inc(s_msg, 1)

            def carry_on(k, lo):
                if isinstance(k, int) and k == 0:
                    V.memset(carry[:, 0:D], 0.0).then_inc(s_fresh, 1)
                    V.memset(carry[:, D:W], 0.0).then_inc(s_fresh, 1)
                    return
                dve.wait_ge(s_carry, lo + 1)
                V.tensor_tensor(carry[:, 0:D].rearrange("p (h f) -> p h f", h=H),
                                carry_ps[:, 0:D].rearrange("p (h f) -> p h f", h=H),
                                bc(fade[0:1, :], [1, H, D // H], 2), ALU.mult).then_inc(s_fresh, 1)
                V.tensor_tensor(carry[:, D:W].rearrange("p (g h) -> p g h", h=H),
                                carry_ps[:, D:W].rearrange("p (g h) -> p g h", h=H),
                                bc(fade[0:1, :], [1, 8 // H, H], 1), ALU.mult).then_inc(s_fresh, 1)

            def onehots(k, b, lo, hi):
                with dve.Fori(lo, hi) as w:
                    dve.wait_ge(s_mm, w + 1)
                    V.tensor_tensor(onehot[:], bc(iota[:], [P, J, WIN], 1), bc(drel[b][:, 1:J + 1], [P, J, WIN], 2),
                                    ALU.is_equal).then_inc(s_hot, 1)
                    V.tensor_scalar(onehot_carry[:], iota[0:1, :], drel[b][0:1, 0:1], None, ALU.is_equal)\
                        .then_inc(s_hot, 1)
                    V.tensor_tensor(pick_last[:], rowid[0:WIN, :], last_rel[b][0:WIN, :], ALU.is_equal).then_inc(s_hot, 1)
                    dve.wait_ge(s_hot, 5 * w + 3)
                    V.tensor_scalar(drel[b][:], drel[b][:], -float(WIN), None, ALU.add).then_inc(s_hot, 1)
                    V.tensor_scalar(last_rel[b][:], last_rel[b][:], -float(WIN), None, ALU.add).then_inc(s_hot, 1)
                    dve.wait_ge(s_hot, 5 * w + 5)

            def segment_maximum(k, s):
                V.tensor_tensor(msg[s % 2][:, :, D + H:W].rearrange("p j h -> p h j"), top[:],
                                bc(cut[:, 1:J + 1], hj, 1), ALU.mult).then_inc(s_fresh, 1)

            def ready(k, s, lo_before):
                maxima(k, s, lo_before)
                if not first_layer:
                    if lo_before is not None:
                        dve.wait_ge(s_mm, lo_before + 1)
                    segment_maximum(k, s)

            scores_and_scans(0, 0)
            scans_across(0, 0)
            ready(0, 0, None)

            def body(k, s, left):
                lo, hi = window_bounds(dve, k)
                t = (s + 1) % RING
                if left:
                    scores_and_scans(k + 1, t)
                products(k, s)
                if left:
                    scans_across(k + 1, t)
                carry_on(k, lo)
                onehots(k, s % 2, lo, hi)
                if left:
                    ready(k + 1, t, lo)

            over_superblocks(dve, body)

        @block.scalar
        def _(act):
            def node_onehots(k, b):
                lo, hi = window_bounds(act, k)
                act.wait_ge(s_dstbc[b], 16 * use(k, b, 2))
                nc.scalar.copy(minus_node[:], keep["minus_node"][0:WIN, bass.ds(k, 1)]).then_inc(s_act, 1)
                act.wait_ge(s_act, lo * 3 + (k + 1))
                with act.Fori(lo, hi) as w:
                    base = act.snap(w * 3 + (k + 1))
                    nc.scalar.activation(dist[:], dst_bc[b][:], ACT.Abs, bias=minus_node[:, 0:1]).then_inc(s_act, 1)
                    act.wait_ge(s_act, base + 1)
                    act.wait_ge(s_spread, w + 1)
                    nc.scalar.activation(node_hot[:], dist[:], ACT.Relu, bias=1.0, scale=-1.0).then_inc(s_node_hot, 1)
                    nc.scalar.activation(minus_node[:], minus_node[:], ACT.Copy, bias=-float(WIN)).then_inc(s_act, 1)
                    act.wait_ge(s_node_hot, w + 1)
                    act.wait_ge(s_act, base + 2)
                    act.sem_inc(s_act, 1)
                act.sem_inc(s_dstbc_used, 1)

            def copy_scores(k, b):
                act.wait_ge(s_attp, k + 1)
                ge(act, s_ae, k)
                nc.scalar.copy(att_T[:], att_ps).then_inc(s_attT, 1)
                ge(act, s_z, 2 * k - 2)
                act.wait_ge(s_ad, k + 1)
                nc.scalar.copy(node_parts[b][:], ad_ps).then_inc(s_node_score, 1)
                act.wait_ge(s_ae, k + 1)
                nc.scalar.copy(edge_score[b][:], ae_ps).then_inc(s_edge_score, 1)

            def exps(k, s, lo_before):
                act.wait_ge(s_z, 2 * k + 2)
                if lo_before is not None:
                    act.wait_ge(s_mm, lo_before + 1)
                ge(act, s_fresh, FRESH * k)
                nc.scalar.activation(msg[s % 2][:, :, D:D + H].rearrange("p j h -> p h j"), z[:], ACT.Exp)\
                    .then_inc(s_exp, 1)
                nc.scalar.activation(fade[:], z_old[:], ACT.Exp).then_inc(s_exp, 1)

            def links(k):
                act.wait_ge(s_ends, k + 1)
                nc.scalar.copy(links_T[:], ends_ps[:, 2:4, :]).then_inc(s_links_T, 1)

            def directed(k, s):
                b = s % 2
                act.wait_ge(s_rows[s], 16 * J * use(k, s, RING))
                ge(act, s_msg, k - 1)
                for j in range(J):
                    nc.scalar.activation(fwd_msg[b][:, j, :], rows[s][:, j, 0:F1], ACT.Copy,
                                         scale=att[s][:, j, 0:1]).then_inc(s_mix, 1)
                    nc.scalar.activation(rev_msg[b][:, j, :], rows[s][:, j, F1:2 * F1], ACT.Copy,
                                         scale=att[s][:, j, 1:2]).then_inc(s_mix, 1)
                act.wait_ge(s_mix, 2 * J * k + 2 * J)
                act.sem_inc(s_att_used, 1)

            if first_layer:
                node_onehots(0, 0)
                copy_scores(0, 0)
            links(0)
            exps(0, 0, None)
            if first_layer:
                node_onehots(1, 1)
                copy_scores(1, 1)
                node_onehots(2, 0)
            else:
                directed(0, 0)

            def body(k, s, left):
                lo, hi = window_bounds(act, k)
                if left:
                    links(k + 1)
                    exps(k + 1, (s + 1) % RING, lo)
                    if not first_layer:
                        directed(k + 1, (s + 1) % RING)
                if first_layer and left >= 2:
                    copy_scores(k + 2, s % 2)
                if first_layer and left >= 3:
                    node_onehots(k + 3, (s + 1) % 2)
                with act.Fori(lo, hi) as w:
                    act.wait_ge(s_mm, w + 2)
                    act.wait_ge(s_out_free, w + 1)
                    act.wait_ge(s_carry, w + 1)
                    nc.scalar.copy(out_rows[:], sums_ps).then_inc(s_out, 1)

            over_superblocks(act, body)

        @block.tensor
        def _(pe):
            pe.wait_ge(s_pool_setup, 4)
            pe.wait_ge(s_dve_setup, 4)
            pe.sem_inc(s_mm, 1)
            pe.sem_inc(s_carry, 1)

            def scores(k, s):
                flat = ad_ps.rearrange("p j h -> p (j h)")
                lo, hi = window_bounds(pe, k)
                ge(pe, s_node_score, k)
                nc.tensor.matmul(flat, zero_row[:, 0:P], zero_row[:, 0:3 * HJ], start=True, stop=False,
                                 skip_group_check=True)
                with pe.Fori(lo, hi) as w:
                    pe.wait_ge(s_node_hot, w + 1)
                    pe.wait_ge(s_adw, 16 * w + 16)
                    hot = node_hot[:].rearrange("p (e j) -> p j e", j=J)
                    for j in range(J):
                        last = nc.tensor.matmul(ad_ps[:, j, :], hot[:, j, :], adst_win[:], start=False, stop=False,
                                                skip_group_check=True)
                    last.then_inc(s_spread, 1)
                nc.tensor.matmul(flat, zero_row[:, 0:P], zero_row[:, 0:3 * HJ], start=False, stop=True,
                                 skip_group_check=True).then_inc(s_ad, 1)
                pe.wait_ge(s_att[s], 16 * use(k, s, RING) + (16 if s == 0 else 0))
                ge(pe, s_attT, k)
                for q in range(J // 2):
                    last = nc.tensor.transpose(att_ps[:, q, :], att[s][:, 2 * q:2 * q + 2, :].rearrange("p j c -> p (j c)"),
                                               ident[:])
                last.then_inc(s_attp, 1)
                pe.wait_ge(s_attT, k + 1)
                ge(pe, s_edge_score, k)
                for q in range(J // 2):
                    last = nc.tensor.matmul(ae_ps[:, 2 * q:2 * q + 2, :].rearrange("p j h -> p (j h)"),
                                            att_T[:, q, :], edge_w[:], start=True, stop=True)
                last.then_inc(s_ae, 1)
                pe.sem_inc(s_att_used, 1)

            def turns(k):
                pe.wait_ge(s_scan, (k + 1) * SCAN)
                nc.tensor.transpose(ends_ps[:, 0, :], fwd[:, :, J - 1], ident[:])
                nc.tensor.transpose(ends_ps[:, 1, :], bwd[:, :, 0], ident[:])
                nc.tensor.transpose(ends_ps[:, 2, :], edge_links[:, 0, :], ident[:])
                nc.tensor.transpose(ends_ps[:, 3, :], edge_links[:, 1, :], ident[:]).then_inc(s_ends, 1)
                pe.wait_ge(s_T, 2 * k + 2)
                pe.sem_inc(s_gate, 1)
                nc.tensor.transpose(back_ps[:, 0, :], fwd_T[:, 0:P], ident[0:H, 0:H])
                nc.tensor.transpose(back_ps[:, 1, :], bwd_T[:, 1:P + 1], ident[0:H, 0:H]).then_inc(s_back, 1)

            if first_layer:
                scores(0, 0)
            turns(0)
            if first_layer:
                scores(1, 1)

            def body(k, s, left):
                lo, hi = window_bounds(pe, k)
                if left:
                    turns(k + 1)
                if first_layer and left >= 2:
                    scores(k + 2, (s + 2) % RING)
                with pe.Fori(lo, hi) as w:
                    pe.wait_ge(s_msg, k + 1)
                    pe.wait_ge(s_hot, 5 * w + 3)
                    pe.wait_ge(s_out_free, w + 1)
                    for j in range(J):
                        nc.tensor.matmul(sums_ps, onehot[:, j, :], msg[s % 2][:, j, :], start=(j == 0), stop=False)
                    nc.tensor.matmul(sums_ps, onehot_carry[:], carry[:], start=False, stop=True).then_inc(s_mm, 1)
                    pe.wait_ge(s_out, w + 1)
                    pe.sem_inc(s_gate, 1)
                    nc.tensor.matmul(carry_ps, pick_last[:], out_rows[:], start=True, stop=True).then_inc(s_carry, 1)

            over_superblocks(pe, body)


def final_stage(nc, x1, acc, gmax, out):
    with ExitStack() as ctx:
        def sb(name, shape, dt=F32):
            return ctx.enter_context(nc.sbuf_tensor("f_" + name, shape, dt))

        def sem(name):
            return ctx.enter_context(nc.semaphore("f_" + name))

        x_in = [sb(f"x{s}", [P, D]) for s in range(RING)]
        sums = [sb(f"sums{s}", [P, W]) for s in range(RING)]
        y = [sb(f"y{s}", [P, D]) for s in range(RING)]
        gap = [sb(f"gap{s}", [P, H1]) for s in range(RING)]
        gap_exp = [sb(f"gap_exp{s}", [P, H1]) for s in range(RING)]
        den = sb("den", [P, 2 * H1])
        agg = sb("agg", [P, D])
        s_in = [sem(f"in{s}") for s in range(RING)]
        s_gap = sem("gap_ready")
        s_exp = sem("exp_ready")
        s_dve = sem("steps")
        s_y = sem("y_ready")
        s_st = [sem(f"stored{s}") for s in range(RING)]
        block = ctx.enter_context(nc.Block())

        @block.sync
        def _(sp):
            def load(t, s, r0):
                ge(sp, s_y, t - RING + 1)
                sp.dma_start(x_in[s][:], x1[bass.ds(r0, P), :]).then_inc(s_in[s], 16)
                sp.dma_start(sums[s][:], acc[bass.ds(r0, P), :]).then_inc(s_in[s], 16)

            over_tiles(sp, [(0, load)])

        @block.vector
        def _(dve):
            c = Chain(dve, s_dve)
            heads = lambda ap: ap.rearrange("p (h f) -> p h f", h=H1)

            def gaps(t, s, r0):
                dve.wait_ge(s_in[s], 32 * use_of(t, s))
                nc.vector.tensor_tensor(gap[s][:], gmax[:], sums[s][:, D + H1:W], ALU.subtract).then_inc(s_gap, 1)

            def add(t, s, r0):
                c.start(3 * t)
                dve.wait_ge(s_exp, t + 1)
                c.done(nc.vector.scalar_tensor_tensor(den[:, 0:H1], gap_exp[s][:], 1e-10, sums[s][:, D:D + H1],
                                                      ALU.mult, ALU.add))
                c.after()
                c.done(nc.vector.reciprocal(den[:, H1:2 * H1], den[:, 0:H1]))
                c.after()
                c.done(nc.vector.tensor_tensor(heads(agg[:]), heads(sums[s][:, 0:D]),
                                               bc(den[:, H1:2 * H1], [P, H1, F1], 2), ALU.mult))
                c.after()
                ge(dve, s_st[s], 16 * (use_of(t, s) - 1))
                nc.vector.tensor_tensor(y[s][:], agg[:], x_in[s][:], ALU.add).then_inc(s_y, 1)

            over_tiles(dve, [(0, gaps), (1, add)])

        @block.scalar
        def _(act):
            def gap_exps(t, s, r0):
                act.wait_ge(s_gap, t + 1)
                ge(act, s_y, t - RING + 1)
                nc.scalar.activation(gap_exp[s][:], gap[s][:], ACT.Exp).then_inc(s_exp, 1)

            def store(t, s, r0):
                act.wait_ge(s_y, t + 1)
                if isinstance(t, int) and t == TILES:
                    act.wait_ge(s_st[(TILES - 1) % RING], 16 * use_of(TILES - 1, (TILES - 1) % RING))
                act.dma_start(out[bass.ds(r0, P), :], y[s][:]).then_inc(s_st[s], 16)

            over_tiles(act, [(0, gap_exps), (2, store)])
            for s in range(RING):
                act.wait_ge(s_st[s], 16 * (-(-(TILES + 1 - s) // RING)))


def gnn_kernel(nc, x, src, dst, edge_attr_2, edge_attr_64, W_w, We_w, a_src, a_dst, a_edge, W_forward, W_reverse,
               attn_forward, out):
    table0 = nc.dram_tensor("table0", [N, W], F32).ap()
    table1 = nc.dram_tensor("table1", [N, W1], F32).ap()
    adst = nc.dram_tensor("adst", [NROWS, 3 * H0], BF16).ap()
    acc0 = nc.dram_tensor("acc0", [NROWS, W], F32).ap()
    acc1 = nc.dram_tensor("acc1", [NROWS, W], F32).ap()
    x1 = nc.dram_tensor("x1", [N, D], F32).ap()
    dst_f = nc.dram_tensor("dst_f", [KSB * SB + J + 2], F32).ap()
    src_pad = nc.dram_tensor("src_pad", [KSB * SB], I32).ap()
    with ExitStack() as ctx:
        def sb(name, shape, dt=F32):
            return ctx.enter_context(nc.sbuf_tensor(name, shape, dt))

        keep = {
            "base_i": sb("base_i", [1, KSB], I32), "win_i": sb("win_i", [1, KSB + 1], I32),
            "base_f": sb("base_f", [P, KSB]), "last_rel": sb("last_rel_all", [P, KSB]),
            "minus_node": sb("minus_node_all", [P, KSB]), "edge_w": sb("edge_w", [P, 2 * H0]),
            "gmax_part": sb("gmax_part", [P, H1]),
        }
        gmax = sb("gmax", [P, H1])
        rings = [[ctx.enter_context(nc.semaphore(f"{name}_in{s}")) for s in range(RING)]
                 for name in ("idx", "dwin", "att", "rows")]
        edge_tables(nc, src, dst, dst_f, src_pad, (acc0, acc1), adst, keep)
        node_stage(nc, 0, x, None, None, table0, adst,
                   {"W": W_w, "We": We_w, "a_src": a_src, "a_dst": a_dst, "a_edge": a_edge}, keep)
        edge_stage(nc, 0, table0, dst_f, src_pad, edge_attr_64, adst, acc0, keep, gmax, rings)
        node_stage(nc, 1, x, acc0, x1, table1, None, {"Wf": W_forward, "Wr": W_reverse, "attn": attn_forward}, keep)
        edge_stage(nc, 1, table1, dst_f, src_pad, edge_attr_2, None, acc1, keep, gmax, rings)
        final_stage(nc, x1, acc1, gmax, out)


_INS = ['x', 'src', 'dst', 'edge_attr_2', 'edge_attr_64', 'L0_gnn_W_w', 'L0_gnn_We_w', 'L0_gnn_a_src', 'L0_gnn_a_dst',
        'L0_gnn_a_edge', 'L1_gnn_W_forward', 'L1_gnn_W_reverse', 'L1_gnn_attn_forward']
_OUTS = [((6250, 256), 'float32')]


def kernel(**inputs):
    import numpy as _np
    import concourse.bacc as _bacc
    from concourse import mybir as _mybir
    from concourse.bass_utils import run_bass_kernel_spmd as _run

    nc = _bacc.Bacc("TRN2", target_bir_lowering=False, num_devices=1)
    arrays, args = {}, []
    for name in _INS:
        a = _np.ascontiguousarray(inputs[name])
        arrays[f"in_{name}_dram"] = a
        args.append(nc.dram_tensor(f"in_{name}_dram", a.shape, _mybir.dt.from_np(a.dtype), kind="ExternalInput").ap())
    for i, (shape, dtype) in enumerate(_OUTS):
        dt = _mybir.dt.from_np(_np.dtype(dtype))
        args.append(nc.dram_tensor(f"out_{i}_dram", shape, dt, kind="ExternalOutput").ap())
    gnn_kernel(nc, *args)
    r = _run(nc, [arrays], core_ids=[0])
    got = tuple(r.results[0][f"out_{i}_dram"] for i in range(len(_OUTS)))
    return got[0]
```

```python
from contextlib import ExitStack

import concourse.bass as bass
from concourse import mybir

F32 = mybir.dt.float32
I32 = mybir.dt.int32
BF16 = mybir.dt.bfloat16
ALU = mybir.AluOpType
ACT = mybir.ActivationFunctionType
AX_X = mybir.AxisListType.X

P = 128
N = 6250
E = 206250
D = 256
EF = 64
EPS = 1e-5
H0, F0 = 8, 32
H1, F1 = 4, 64

RING = 4
J = 14
SB = P * J
KSB = -(-E // SB)
KSB += -KSB % RING
FRONT = KSB * SB - E
assert 0 < FRONT < SB
W = D + 8
W1 = 2 * F1 + 2 * H1
WIN = 64
MAX_WINDOWS = KSB + N // WIN + 1
NROWS = 6400
TILES = N // P
LAST0 = N - P
BIG = 1.0e30
NO_NODE = -1.0


def ge(eng, sem, value):
    if not isinstance(value, int) or value > 0:
        eng.wait_ge(sem, value)


def bc(ap, shape, *axes):
    for a in axes:
        ap = ap.unsqueeze(a)
    return ap.to_broadcast(shape)


class Chain:

    def __init__(self, eng, sem):
        self.eng, self.sem, self.base, self.n = eng, sem, 0, 0

    def start(self, base):
        self.base, self.n = base, 0

    def done(self, ins):
        self.n += 1
        ins.then_inc(self.sem, 1)
        return self.n

    def after(self, n=None):
        ge(self.eng, self.sem, self.base + (self.n if n is None else n))


def bank(nc, ctx, name, shape):
    size = 1
    for n in shape[1:]:
        size *= n
    whole = ctx.enter_context(nc.psum_tensor(name, [P, -(-size // 512) * 512], F32))
    view = whole[0:shape[0], 0:size]
    if len(shape) == 2:
        return view
    axes = "abcd"[:len(shape) - 1]
    return view.rearrange(f"p ({' '.join(axes)}) -> p {' '.join(axes)}", **dict(zip(axes, shape[1:])))


def make_identity(nc, pool, ident, sem):
    nc.gpsimd.memset(ident[:], 0.0).then_inc(sem, 1)
    pool.wait_ge(sem, 1)
    nc.gpsimd.affine_select(out=ident[:], in_=ident[:], compare_op=ALU.not_equal, fill=1.0, base=0,
                            pattern=[[-1, P]], channel_multiplier=1).then_inc(sem, 1)


def edge_tables(nc, src, dst, dst_f, src_pad, adst, keep):
    with ExitStack() as ctx:
        def sb(name, shape, dt=F32):
            return ctx.enter_context(nc.sbuf_tensor(name, shape, dt))

        def sem(name):
            return ctx.enter_context(nc.semaphore(name))

        R = 125
        BC_STEP = 10
        edges = sb("et_edges", [R, E // R], I32)
        edges_f = sb("et_edges_f", [R, E // R])
        pad_f = sb("et_pad_f", [1, FRONT + 1])
        pad_i = sb("et_pad_i", [1, FRONT], I32)
        zero_bf = sb("et_zero_bf", [50, 9 * H0], BF16)
        ends_i = sb("et_ends_i", [1, 2 * KSB], I32)
        ends_f = sb("et_ends_f", [1, 2 * KSB])
        span_i = sb("et_span_i", [1, 2 * KSB], I32)
        span_f = sb("et_span_f", [1, 2 * KSB])
        ones = sb("et_ones", [1, KSB])
        ones_row = sb("et_ones_row", [1, P])
        rowid = sb("et_rowid", [P, 1])
        ends_ps = ctx.enter_context(nc.psum_tensor("et_ends_ps", [P, 2 * KSB], F32))
        s_dst = sem("et_dst")
        s_ends = sem("et_ends")
        s_set = sem("et_set")
        s_dve = sem("et_dve")
        s_pads = sem("et_pads")
        s_float = sem("et_float")
        s_bc = sem("et_bc")
        s_rowid = sem("et_rowid_sem")
        s_out = sem("et_out")
        block = ctx.enter_context(nc.Block())

        @block.sync
        def _(sp):
            sp.dma_start(edges[:], dst.rearrange("(p e) -> p e", p=R)).then_inc(s_dst, 16)
            sp.wait_ge(s_set, 1)
            with nc.allow_non_contiguous_dma(reason="one element per superblock"):
                body = dst[SB - FRONT:E]
                sp.dma_start(ends_i[:, 1:KSB], body.rearrange("(k e) -> k e", e=SB)[:, 0:1]
                             .rearrange("k e -> e k")).then_inc(s_ends, 16)
                sp.dma_start(ends_i[:, KSB + 1:2 * KSB], body.rearrange("(k e) -> k e", e=SB)[:, SB - 1:SB]
                             .rearrange("k e -> e k")).then_inc(s_ends, 16)
            sp.dma_start(ends_i[:, KSB:KSB + 1], dst[SB - FRONT - 1:SB - FRONT].unsqueeze(0)).then_inc(s_ends, 16)
            sp.dma_start(src_pad[FRONT:FRONT + E].rearrange("(p e) -> p e", p=R),
                         src.rearrange("(p e) -> p e", p=R)).then_inc(s_out, 16)
            sp.wait_ge(s_pads, 3)
            sp.dma_start(src_pad[0:FRONT].unsqueeze(0), pad_i[:]).then_inc(s_out, 16)
            sp.dma_start(dst_f[0:FRONT + 1].unsqueeze(0), pad_f[:]).then_inc(s_out, 16)
            sp.dma_start(dst_f[FRONT + 1 + E:FRONT + 1 + E + J + 1].unsqueeze(0), pad_f[:, 0:J + 1]).then_inc(s_out, 16)
            n_out = 4
            sp.dma_start(adst[N:NROWS, :].rearrange("(p r) c -> p (r c)", p=50), zero_bf[0:50, :]).then_inc(s_out, 16)
            sp.wait_ge(s_float, 1)
            sp.dma_start(dst_f[FRONT + 1:FRONT + 1 + E].rearrange("(p e) -> p e", p=R), edges_f[:]).then_inc(s_out, 16)
            n_out += 2
            sp.wait_ge(s_out, 16 * n_out)

        @block.gpsimd
        def _(pool):
            nc.gpsimd.iota(rowid[:], pattern=[[0, 1]], base=0, channel_multiplier=1,
                           allow_small_or_imprecise_dtypes=True).then_inc(s_rowid, 1)

        @block.vector
        def _(dve):
            step = Chain(dve, s_dve)
            nc.vector.memset(ends_i[:], 0).then_inc(s_set, 1)
            nc.vector.memset(pad_f[:], NO_NODE).then_inc(s_pads, 1)
            nc.vector.memset(pad_i[:], 0).then_inc(s_pads, 1)
            nc.vector.memset(zero_bf[:], 0.0).then_inc(s_pads, 1)
            step.done(nc.vector.memset(ones[:], 1.0))
            step.done(nc.vector.memset(ones_row[:], 1.0))
            step.done(nc.vector.memset(keep["win_i"][:], 0))
            dve.wait_ge(s_dst, 16)
            nc.vector.tensor_copy(edges_f[:], edges[:]).then_inc(s_float, 1)
            dve.wait_ge(s_ends, 48)
            step.done(nc.vector.tensor_copy(keep["base_i"][:], ends_i[:, 0:KSB]))
            step.done(nc.vector.tensor_copy(ends_f[:, 0:KSB], ends_i[:, 0:KSB]))
            step.after()
            step.done(nc.vector.tensor_tensor(span_i[:, 0:KSB], ends_i[:, KSB:2 * KSB], ends_i[:, 0:KSB], ALU.subtract))
            step.after()
            step.done(nc.vector.tensor_single_scalar(span_i[:, KSB:2 * KSB], span_i[:, 0:KSB], WIN.bit_length() - 1, op=ALU.arith_shift_right))
            step.after()
            step.done(nc.vector.tensor_copy(span_f[:, 0:KSB], span_i[:, KSB:2 * KSB]))
            step.done(nc.vector.tensor_copy(span_f[:, KSB:2 * KSB], span_i[:, 0:KSB]))
            step.after()
            to_bc = step.done(nc.vector.scalar_tensor_tensor(ends_f[:, KSB:2 * KSB], span_f[:, 0:KSB], -float(WIN),
                                                             span_f[:, KSB:2 * KSB], ALU.mult, ALU.add))
            assert to_bc == BC_STEP
            step.after()
            step.done(nc.vector.tensor_scalar(span_f[:, KSB:2 * KSB], span_f[:, 0:KSB], 1.0, None, ALU.add))
            step.after()
            step.done(nc.vector.tensor_tensor_scan(span_f[:, 0:KSB], ones[:], span_f[:, KSB:2 * KSB], 0.0,
                                                   ALU.mult, ALU.add))
            step.after()
            step.done(nc.vector.tensor_copy(keep["win_i"][:, 1:KSB + 1], span_f[:, 0:KSB]))
            dve.wait_ge(s_bc, 1)
            dve.wait_ge(s_rowid, 1)
            step.done(nc.vector.tensor_copy(keep["base_f"][:], ends_ps[:, 0:KSB]))
            step.after()
            step.done(nc.vector.tensor_copy(keep["last_rel"][:], ends_ps[:, KSB:2 * KSB]))
            step.done(nc.vector.tensor_scalar(keep["minus_node"][:], keep["base_f"][:], rowid[:, 0:1], -1.0,
                                              ALU.add, ALU.mult))
            step.after()

        @block.tensor
        def _(pe):
            pe.wait_ge(s_dve, BC_STEP)
            nc.tensor.matmul(ends_ps[:], ones_row[:], ends_f[:], start=True, stop=True).then_inc(s_bc, 1)


def over_tiles(eng, stages):
    lags = max(lag for lag, _ in stages)
    assert lags <= RING

    def step(u, s):
        for lag, fn in stages:
            t = u - lag
            if not isinstance(u, int):
                fn(t, (s - lag) % RING, t * P)
            elif 0 <= t <= TILES:
                fn(t, t % RING, t * P if t < TILES else LAST0)

    first, turns = RING, (TILES - RING) // RING
    for u in range(first):
        step(u, u)
    with eng.Fori(1, 1 + turns) as i:
        for s in range(RING):
            step(RING * i + s, s)
    for u in range(first + RING * turns, TILES + 1 + lags):
        step(u, u % RING)


def use_of(t, s):
    return t // RING + 1 if isinstance(t, int) else (t - s) // RING + 1


T = TILES + 1
CHUNKS = [(n * (TILES // 4), (n + 1) * (TILES // 4) + (n == 3)) for n in range(4)]


def move_chunk(eng, n, tiles, rows, sem, to_dram=False):
    a, b = CHUNKS[n]
    b = min(b, TILES)
    dram = rows[a * P:b * P, :].rearrange("(t p) c -> p t c", p=P)
    tail = rows[LAST0:N, :]
    if to_dram:
        eng.dma_start(dram, tiles[:, a:b]).then_inc(sem, 16)
    else:
        eng.dma_start(tiles[:, a:b], dram).then_inc(sem, 16)
    if n < 3:
        return 16
    if to_dram:
        eng.wait_ge(sem, 64)
        eng.dma_start(tail, tiles[:, TILES]).then_inc(sem, 16)
    else:
        eng.dma_start(tiles[:, TILES], tail).then_inc(sem, 16)
    return 32


def node_stage(nc, layer, x, acc0, x1, table, adst, weights, keep, clear=()):
    second = layer == 1
    cols = W + H0 if not second else W1
    width = W if not second else W1
    tag = f"n{layer}_"
    with ExitStack() as ctx:
        def sb(name, shape, dt=F32):
            return ctx.enter_context(nc.sbuf_tensor(tag + name, shape, dt))

        def sem(name):
            return ctx.enter_context(nc.semaphore(tag + name))

        def ps(name, shape):
            return bank(nc, ctx, tag + name, shape)

        ident = sb("ident", [P, P])
        rhs = sb("rhs", [P, 2, cols])
        xs = sb("xs", [P, T, D])
        stats = sb("stats", [P, T, nc.vector.BN_STATS_DIM])
        mean = sb("mean", [P, T])
        half_gap = sb("half_gap", [P, T])
        moment = sb("moment", [P, T])
        var_eps = sb("var_eps", [P, T])
        std = sb("std", [P, T])
        rstd = sb("rstd", [P, T])
        h = [sb(f"h{s}", [P, D]) for s in range(RING)]
        hT = [sb(f"hT{s}", [P, 2, P]) for s in range(RING)]
        row = [sb(f"row{s}", [P, width]) for s in range(RING)]
        hT_ps = [ps(f"hT_ps{b}", [P, 2, P]) for b in range(2)]
        row_ps = [ps(f"row_ps{b}", [P, cols]) for b in range(2)]
        w_ps = ps("w_ps", [P, 512])
        if not second:
            w_in = sb("w_in", [P, 2, D])
            a_row = sb("a_row", [P, 3, D])
            we = sb("we", [P, D])
            zero = sb("zero", [P, W])
            prod = sb("prod", [P, D])
            score = sb("score", [P, T, H0])
            rest = sb("rest", [P, 2, T, H0])
            parts = sb("parts", [P, T, 3, H0], BF16)
        else:
            w_in = sb("w_in", [F1, 2, D])
            a_row = sb("a_row", [F1, H1])
            sums = sb("sums", [P, T, W])
            den = sb("den", [P, T, H0])
            rden = sb("rden", [P, T, H0])
            low = [sb(f"low{b}", [P, CHUNKS[3][1] - CHUNKS[3][0], D]) for b in range(2)]

        s_id = sem("id")
        s_w = sem("w")
        s_wdve = sem("wdve")
        s_rhs = sem("rhs_ready")
        s_x = [sem(f"x_in{n}") for n in range(4)]
        s_stats = sem("stats_ready")
        s_stat = sem("stat_steps")
        s_std = sem("std_ready")
        s_rstd = sem("rstd_ready")
        s_h = sem("h_ready")
        s_hTp = sem("hT_turned")
        s_hT = sem("hT_ready")
        s_rowp = sem("row_summed")
        s_row = sem("row_ready")
        s_st = [sem(f"stored{s}") for s in range(RING)]
        if not second:
            s_split = sem("split_steps")
            s_cleared = sem("sums_cleared")
            s_zero = sem("zero_ready")
            s_adst = sem("adst_stored")
        else:
            s_wps = sem("wps")
            s_sums = [sem(f"sums_in{n}") for n in range(4)]
            s_den = sem("den_steps")
            s_agg = sem("agg_ready")
            s_low = sem("low_ready")
            s_exp = sem("exp_ready")
            s_upd = sem("update_ready")
            s_new = sem("x_new_ready")
            s_x1 = sem("x1_stored")
        block = ctx.enter_context(nc.Block())

        @block.sync
        def _(sp):
            if not second:
                for n in range(4):
                    move_chunk(sp, n, xs, x, s_x[n])
                sp.dma_start(w_in[:], weights["W"].rearrange("(c p) n -> p c n", p=P)).then_inc(s_w, 16)
                for n, a in enumerate(("a_src", "a_dst", "a_edge")):
                    sp.dma_start(a_row[:, n, :], bc(weights[a].rearrange("h f -> (h f)"), [P, D], 0)).then_inc(s_w, 16)
                for half in range(2):
                    sp.dma_start(we[EF * half:EF * half + EF, :], weights["We"]).then_inc(s_w, 16)
            else:
                for n in range(4):
                    move_chunk(sp, n, sums, acc0, s_sums[n])
                    move_chunk(sp, n, xs, x, s_x[n])
                sp.dma_start(w_in[:, 0, :], weights["Wf"]).then_inc(s_w, 16)
                sp.dma_start(w_in[:, 1, :], weights["Wr"]).then_inc(s_w, 16)
                with nc.allow_non_contiguous_dma(reason="256 weights, turned"):
                    sp.dma_start(a_row[:], weights["attn"][0].rearrange("h f -> f h")).then_inc(s_w, 16)
                for n in range(4):
                    sp.wait_ge(s_new, n + 1)
                    move_chunk(sp, n, xs, x1, s_x1, to_dram=True)

            def store(t, s, r0):
                if isinstance(t, int) and t == TILES:
                    sp.wait_ge(s_st[(TILES - 1) % RING], 16 * use_of(TILES - 1, (TILES - 1) % RING))
                sp.wait_ge(s_row, t + 1)
                sp.dma_start(table[bass.ds(r0, P), :], row[s][:, 0:width]).then_inc(s_st[s], 16)

            over_tiles(sp, [(0, store)])
            if not second:
                sp.wait_ge(s_split, 5)
                with nc.allow_non_contiguous_dma(reason="24 parts per node"):
                    for n in range(4):
                        move_chunk(sp, n, parts[:].rearrange("p t q h -> p t (q h)"), adst, s_adst, to_dram=True)
                sp.wait_ge(s_adst, 80)
            else:
                sp.wait_ge(s_x1, 80)
            for s in range(RING):
                sp.wait_ge(s_st[s], 16 * (-(-(T - s) // RING)))

        @block.gpsimd
        def _(pool):
            make_identity(nc, pool, ident, s_id)
            if not second:
                nc.gpsimd.memset(zero[:], 0.0).then_inc(s_zero, 1)
                pool.wait_ge(s_zero, 1)
                for a in clear:
                    pool.dma_start(a.rearrange("(p r) c -> p r c", p=P),
                                   bc(zero[:], [P, NROWS // P, W], 1)).then_inc(s_cleared, 16)
                pool.wait_ge(s_cleared, 16 * len(clear))

        @block.vector
        def _(dve):
            V = nc.vector

            def statistics(n):
                a, b = CHUNKS[n]
                with dve.Fori(a // 4, b // 4) as i:
                    for q in range(4):
                        V.bn_stats(stats[:, bass.ds(4 * i + q, 1), :].rearrange("p o c -> p (o c)"),
                                   xs[:, bass.ds(4 * i + q, 1), :].rearrange("p o d -> p (o d)")).then_inc(s_stats, 1)
                if b > TILES:
                    V.bn_stats(stats[:, TILES, :], xs[:, TILES, :]).then_inc(s_stats, 1)

            if not second:
                for n in range(4):
                    dve.wait_ge(s_x[n], 32 if n == 3 else 16)
                    statistics(n)
            else:
                den_c = Chain(dve, s_den)

                def aggregate(n):
                    a, b = CHUNKS[n]
                    dve.wait_ge(s_sums[n], 32 if n == 3 else 16)
                    den_c.done(V.tensor_scalar(den[:, a:b], sums[:, a:b, D:W], 1e-30, None, ALU.max))
                    den_c.after()
                    den_c.done(V.reciprocal(rden[:, a:b], den[:, a:b]))
                    den_c.after()
                    heads = sums[:, a:b, 0:D].rearrange("p t (h f) -> p t h f", h=H0)
                    V.tensor_tensor(heads, heads, bc(rden[:, a:b], [P, b - a, H0, F0], 3), ALU.mult).then_inc(s_agg, 1)

                def update(n):
                    a, b = CHUNKS[n]
                    v = sums[:, a:b, 0:D]
                    dve.wait_ge(s_x[n], 32 if n == 3 else 16)
                    dve.wait_ge(s_low, n + 1)
                    V.scalar_tensor_tensor(v, v, 0.0, xs[:, a:b], ALU.max, ALU.add).then_inc(s_upd, 1)
                    dve.wait_ge(s_exp, n + 1)
                    dve.wait_ge(s_upd, n + 1)
                    V.scalar_tensor_tensor(xs[:, a:b], low[n % 2][:, 0:b - a], -1.0, v, ALU.add, ALU.add)\
                        .then_inc(s_new, 1)
                    dve.wait_ge(s_new, n + 1)
                    statistics(n)

                for n in range(5):
                    if n < 4:
                        aggregate(n)
                    if n > 0:
                        update(n - 1)
            c = Chain(dve, s_stat)
            dve.wait_ge(s_stats, T)
            c.done(V.tensor_tensor(mean[:], stats[:, :, 1], stats[:, :, 4], ALU.add))
            c.done(V.tensor_tensor(half_gap[:], stats[:, :, 1], stats[:, :, 4], ALU.subtract))
            c.done(V.tensor_tensor(moment[:], stats[:, :, 2], stats[:, :, 5], ALU.add))
            c.after()
            c.done(V.tensor_scalar(mean[:], mean[:], 0.5, None, ALU.mult))
            c.done(V.tensor_tensor(half_gap[:], half_gap[:], half_gap[:], ALU.mult))
            c.after()
            c.done(V.scalar_tensor_tensor(moment[:], half_gap[:], D / 4.0, moment[:], ALU.mult, ALU.add))
            c.after()
            c.done(V.tensor_scalar(var_eps[:], moment[:], 1.0 / D, EPS, ALU.mult, ALU.add))
            dve.wait_ge(s_std, 1)
            V.reciprocal(rstd[:], std[:]).then_inc(s_rstd, 1)

            step = Chain(dve, s_wdve)
            if not second:
                dve.wait_ge(s_w, 96)
                step.done(V.memset(keep["edge_w"][:], 0.0))
                for c in range(2):
                    V.tensor_copy(rhs[:, c, 0:D], w_in[:, c, :]).then_inc(s_rhs, 1)
                    for n in range(2):
                        step.after()
                        step.done(V.tensor_tensor(prod[:], w_in[:, c, :], a_row[:, n, :], ALU.mult))
                        step.after()
                        step.done(V.tensor_reduce(rhs[:, c, D + n * H0:D + (n + 1) * H0],
                                                  prod[:].rearrange("p (h f) -> p h f", h=H0), AX_X, ALU.add))
                step.after()
                step.done(V.tensor_tensor(prod[:], we[:], a_row[:, 2, :], ALU.mult))
                step.after()
                for half in range(2):
                    q = slice(EF * half, EF * half + EF)
                    step.done(V.tensor_reduce(keep["edge_w"][q, H0 * half:H0 * half + H0],
                                              prod[q, :].rearrange("p (h f) -> p h f", h=H0), AX_X, ALU.add))
                step.after()
                dve.sem_inc(s_rhs, 1)
            else:
                dve.wait_ge(s_wps, 2)
                V.tensor_copy(rhs[:].rearrange("p c n -> p (c n)"), w_ps[:, 0:2 * W1]).then_inc(s_rhs, 3)
            dve.wait_ge(s_rstd, 1)

            def normalize(t, s, r0):
                ge(dve, s_hTp, t - RING + 1)
                V.tensor_scalar(h[s][:], xs[:, bass.ds(t, 1), :].rearrange("p o d -> p (o d)"), mean[:, bass.ds(t, 1)],
                                rstd[:, bass.ds(t, 1)], ALU.subtract, ALU.mult).then_inc(s_h, 1)

            over_tiles(dve, [(0, normalize)])
            if not second:
                c = Chain(dve, s_split)
                dve.wait_ge(s_row, T)
                c.done(V.tensor_copy(parts[:, :, 0], score[:]))
                c.after()
                c.done(V.tensor_tensor(rest[:, 0], score[:], parts[:, :, 0], ALU.subtract))
                c.after()
                c.done(V.tensor_copy(parts[:, :, 1], rest[:, 0]))
                c.after()
                c.done(V.tensor_tensor(rest[:, 1], rest[:, 0], parts[:, :, 1], ALU.subtract))
                c.after()
                c.done(V.tensor_copy(parts[:, :, 2], rest[:, 1]))

        @block.tensor
        def _(pe):
            pe.wait_ge(s_id, 2)
            if second:
                pe.wait_ge(s_w, 48)
                for c in range(2):
                    cs = slice(c * P, (c + 1) * P)
                    o = c * W1
                    for n in range(2):
                        nc.tensor.transpose(w_ps[:, o + n * F1:o + (n + 1) * F1], w_in[:, n, cs], ident[0:F1, 0:F1])
                        last = nc.tensor.matmul(w_ps[:, o + 2 * F1 + n * H1:o + 2 * F1 + (n + 1) * H1],
                                                w_in[:, n, cs], a_row[:], start=True, stop=True)
                    last.then_inc(s_wps, 1)
            pe.wait_ge(s_rhs, 3)

            def turn(t, s, r0):
                pe.wait_ge(s_h, t + 1)
                ge(pe, s_hT, t - 1)
                for c in range(2):
                    last = nc.tensor.transpose(hT_ps[s % 2][:, c, :], h[s][:, c * P:(c + 1) * P], ident[:])
                last.then_inc(s_hTp, 1)

            def product(t, s, r0):
                pe.wait_ge(s_hT, t + 1)
                ge(pe, s_row, t - 1)
                for c in range(2):
                    last = nc.tensor.matmul(row_ps[s % 2], hT[s][:, c, :], rhs[:, c, :], start=(c == 0), stop=(c == 1))
                last.then_inc(s_rowp, 1)

            over_tiles(pe, [(0, turn), (1, product)])

        @block.scalar
        def _(act):
            if second:
                for n in range(4):
                    a, b = CHUNKS[n]
                    q = low[n % 2][:, 0:b - a]
                    act.wait_ge(s_agg, n + 1)
                    if n >= 2:
                        act.wait_ge(s_new, n - 1)
                    nc.scalar.activation(q, sums[:, a:b, 0:D], ACT.Relu, scale=-1.0).then_inc(s_low, 1)
                    act.wait_ge(s_low, n + 1)
                    nc.scalar.activation(q, q, ACT.Exp, scale=-1.0).then_inc(s_exp, 1)
            act.wait_ge(s_stat, 7)
            nc.scalar.activation(std[:], var_eps[:], ACT.Sqrt).then_inc(s_std, 1)

            def relu(t, s, r0):
                act.wait_ge(s_hTp, t + 1)
                ge(act, s_rowp, t - RING + 1)
                nc.scalar.activation(hT[s][:], hT_ps[s % 2], ACT.Relu).then_inc(s_hT, 1)

            def copy_row(t, s, r0):
                act.wait_ge(s_rowp, t + 1)
                ge(act, s_st[s], 16 * (use_of(t, s) - 1))
                if not second:
                    nc.scalar.copy(score[:, bass.ds(t, 1), :].rearrange("p o h -> p (o h)"), row_ps[s % 2][:, W:W + H0])
                nc.scalar.copy(row[s][:], row_ps[s % 2][:, 0:width]).then_inc(s_row, 1)

            over_tiles(act, [(0, relu), (1, copy_row)])


def edge_stage(nc, layer, table, dst_f, src_pad, attr, adst, acc, keep, gmax, rings):
    first_layer = layer == 0
    H = H0 if first_layer else H1
    TW = W if first_layer else W1
    HJ = H * J
    AF = EF if first_layer else 2
    tag = f"e{layer}_"
    with ExitStack() as ctx:
        def sb(name, shape, dt=F32):
            return ctx.enter_context(nc.sbuf_tensor(tag + name, shape, dt))

        def sem(name):
            return ctx.enter_context(nc.semaphore(tag + name))

        def ps(name, shape):
            return bank(nc, ctx, tag + name, shape)

        ident = sb("ident", [P, P])
        iota = sb("iota", [P, WIN])
        rowid = sb("rowid", [P, 1])
        zero_row = sb("zero_row", [1, 512], BF16)
        idx = [sb(f"idx{s}", [P, J], I32) for s in range(RING)]
        dwin = [sb(f"dwin{s}", [P, J + 2]) for s in range(RING)]
        att = [sb(f"att{s}", [P, J, AF]) for s in range(RING)]
        rows = [sb(f"rows{s}", [P, J, TW]) for s in range(RING)]
        drel = [sb(f"drel{s}", [P, J + 1]) for s in range(RING)]
        headmask = [sb(f"headmask{b}", [P, J]) for b in range(2)]
        tailmask = [sb(f"tailmask{b}", [P, J]) for b in range(2)]
        cut = [sb(f"cut{b}", [P, J + 1]) for b in range(2)]
        link = sb("link", [P, HJ + 1])
        score = [sb(f"score{b}", [P, H, J]) for b in range(2)]
        fwd = [sb(f"fwd{b}", [P, H, J]) for b in range(2)]
        bwd = [sb(f"bwd{b}", [P, H, J]) for b in range(2)]
        edge_links = sb("edge_links", [P, 2, H])
        links_T = sb("links_T", [H, 2, P])
        fwd_T = sb("fwd_T", [H, P + 1])
        bwd_T = sb("bwd_T", [H, P + 1])
        local = sb("local", [P, H, J])
        from_prev = sb("from_prev", [P, H, J])
        from_next = sb("from_next", [P, H, J])
        across = sb("across", [P, H, J])
        top = sb("top", [P, H, J])
        z = sb("z", [P, H, J])
        z_old = sb("z_old", [P, H])
        fade = sb("fade", [P, H])
        msg = [sb(f"msg{b}", [P, J, W]) for b in range(2)]
        onehot = [sb(f"onehot{b}", [P, J, WIN]) for b in range(2)]
        onehot_carry = [sb(f"onehot_carry{b}", [1, WIN]) for b in range(2)]
        pick_last = [sb(f"pick_last{b}", [WIN, 1]) for b in range(2)]
        carry = sb("carry", [1, W])
        out_rows = sb("out_rows", [WIN, W])

        sums_ps = ps("sums_ps", [WIN, W])
        ends_ps = ps("ends_ps", [H, 4, P])
        back_ps = ps("back_ps", [P, 2, H])
        carry_ps = ps("carry_ps", [1, W])
        if first_layer:
            old = sb("old", [P, H])
            both = sb("both", [P, 2, H, J])
            both_l = sb("both_l", [P, 2, H, J])
            old_l = sb("old_l", [P, H])
            att_T = sb("att_T", [P, J // 2, P])
            dst_bc = [sb(f"dst_bc{b}", [WIN, SB]) for b in range(2)]
            dist = sb("dist", [WIN, SB])
            node_hot = sb("node_hot", [WIN, SB], BF16)
            minus_node = sb("minus_node", [WIN, 1])
            adst_win = sb("adst_win", [WIN, 3 * H0], BF16)
            att_ps = ps("att_ps", [P, J // 2, P])
            ae_ps = ps("ae_ps", [P, J, H0])
            ad_ps = ps("ad_ps", [P, J, 3 * H0])
            edge_w = keep["edge_w"]
            edge_score = [sb(f"edge_score{b}", [P, J, H0]) for b in range(2)]
            node_parts = [sb(f"node_parts{s}", [P, J, 3 * H0]) for s in range(RING)]
            node_two = sb("node_two", [P, H, J])
            node_score = sb("node_score", [P, H, J])
        else:
            t0 = sb("t0", [P, H, J])
            t1 = sb("t1", [P, H, J])
            t2 = sb("t2", [P, H, J])
            kmax = sb("kmax", [P, H])
            fwd_msg = [sb(f"fwd_msg{b}", [P, J, F1]) for b in range(2)]
            rev_msg = [sb(f"rev_msg{b}", [P, J, F1]) for b in range(2)]
            mix = sb("mix", [P, J, F1])

        s_setup = sem("setup")
        s_dve_setup = sem("dve_setup")
        s_pool_setup = sem("pool_setup")
        s_idx, s_dwin, s_att, s_rows = rings
        s_go = sem("slot_granted")
        s_gate = sem("gate")
        s_att_used = sem("att_used")
        s_scan = sem("scan_steps")
        s_max = sem("max_steps")
        s_links_T = sem("links_T_ready")
        s_ends = sem("ends_turned")
        s_T = sem("scans_T_ready")
        s_back = sem("back_turned")
        s_z = sem("z_ready")
        s_exp = sem("exp_ready")
        s_msg = sem("msg_ready")
        s_fresh = sem("carry_ready")
        s_hot = sem("onehot_ready")
        s_next_hot = sem("next_onehot_ready")
        s_mm = sem("window_summed")
        s_out = sem("out_rows_ready")
        s_carry = sem("carry_picked")
        s_stored = sem("stored")
        if first_layer:
            s_dstbc = [sem(f"dst_bc_in{b}") for b in range(2)]
            s_adw = sem("adst_win_in")
            s_dstbc_used = sem("dst_bc_used")
            s_act = sem("act")
            s_node_hot = sem("node_hot_ready")
            s_spread = sem("adst_spread")
            s_ad = sem("ad_ready")
            s_attp = sem("att_turned")
            s_attT = sem("att_T_ready")
            s_ae = sem("ae_ready")
            s_edge_score = sem("edge_score_ready")
            s_node_score = sem("node_parts_ready")
        else:
            s_mix = sem("fwd_rev_ready")
            s_prod = sem("product_steps")
        block = ctx.enter_context(nc.Block())
        SCAN = 10 if first_layer else 16
        MAX = 13 if first_layer else 6
        FRESH = 2 if first_layer else 3

        def over_superblocks(eng, stages):
            def cycle(u, s):
                for lead, fn in stages:
                    if not isinstance(u, int) or 0 <= u + lead < KSB:
                        fn(u + lead, (s + lead) % RING)

            ahead = max(lead for lead, _ in stages)
            turns = KSB // RING - max(1, -(-ahead // RING))
            for u in range(-ahead, RING):
                cycle(u, u % RING)
            with eng.Fori(1, turns) as i:
                for s in range(RING):
                    cycle(RING * i + s, s)
            for u in range(RING * turns, KSB):
                cycle(u, u % RING)

        def use(k, s, ring):
            before = 0 if first_layer else KSB // ring
            return before + (k // ring + 1 if isinstance(k, int) else (k - s) // ring + 1)

        def att_landed(k, s):
            return 16 * use(k, s, RING) + (16 * (layer + 1) if s == 0 else 0)

        def window_bounds(eng, k):
            lo = eng.value_load(keep["win_i"][0:1, bass.ds(k, 1)], min_val=0, max_val=MAX_WINDOWS)
            hi = eng.value_load(keep["win_i"][0:1, bass.ds(k + 1, 1)], min_val=1, max_val=MAX_WINDOWS)
            return lo, hi

        def window_row(eng, base, w, lo):
            return nc.s_assert_within(eng.snap(base + (w - lo) * WIN), 0, NROWS - WIN, skip_runtime_bounds_check_because=
                                      "a window begins at most WIN after its superblock's last destination")

        @block.sync
        def _(sp):
            def load(k, s):
                n = use(k, s, RING)
                e0 = SB * k
                ge(sp, s_rows[s], 16 * J * (n - 1))
                sp.dma_start(idx[s][:], src_pad[bass.ds(e0, SB)].rearrange("(p j) -> p j", p=P)).then_inc(s_idx[s], 16)
                ge(sp, s_scan, (k - RING + 1) * SCAN)
                sp.dma_start(dwin[s][:, 0:J], dst_f[bass.ds(e0, SB)].rearrange("(p j) -> p j", p=P))\
                  .then_inc(s_dwin[s], 16)
                sp.dma_start(dwin[s][:, J:J + 2], dst_f[bass.ds(e0 + J, SB)].rearrange("(p j) -> p j", p=P)[:, 0:2])\
                  .then_inc(s_dwin[s], 16)
                ge(sp, s_att_used, k - RING + 1)
                if isinstance(k, int) and k == 0:
                    p0, j0 = FRONT // J, FRONT % J
                    part = J - j0
                    sp.wait_ge(s_setup, 1)
                    sp.dma_start(att[s][p0:p0 + 1, j0:J, :], attr[0:part, :].unsqueeze(0)).then_inc(s_att[s], 16)
                    sp.dma_start(att[s][p0 + 1:P, :, :], attr[part:SB - FRONT, :].rearrange("(p j) c -> p j c", j=J))\
                      .then_inc(s_att[s], 16)
                else:
                    sp.dma_start(att[s][:], attr[bass.ds(e0 - FRONT, SB), :].rearrange("(p j) c -> p j c", j=J))\
                      .then_inc(s_att[s], 16)

            def load_dst_bc(k, s):
                ge(sp, s_dstbc_used, k - 1)
                b = s % 2
                sp.dma_start(dst_bc[b][:], bc(dst_f[bass.ds(SB * k + 1, SB)], [WIN, SB], 0)).then_inc(s_dstbc[b], 16)

            def first_adst(k, s):
                base = sp.value_load(keep["base_i"][0:1, bass.ds(k, 1)], min_val=0, max_val=N - 1)
                lo, _ = window_bounds(sp, k)
                if not isinstance(k, int) or k > 0:
                    sp.wait_ge(s_adw, (lo + k) * 16)
                sp.dma_start(adst_win[:], adst[bass.ds(base, WIN), :]).then_inc(s_adw, 16)

            def next_adst(k, s):
                base = sp.value_load(keep["base_i"][0:1, bass.ds(k, 1)], min_val=0, max_val=N - 1)
                lo, hi = window_bounds(sp, k)
                with sp.Fori(lo, hi) as w:
                    row = window_row(sp, base, w + 1, lo)
                    sp.wait_ge(s_adw, (w + (k + 1)) * 16)
                    sp.sem_inc(s_gate, 1)
                    sp.wait_ge(s_spread, w + 1)
                    sp.dma_start(adst_win[:], adst[bass.ds(row, WIN), :]).then_inc(s_adw, 16)

            over_superblocks(sp, [(5, load)] + (
                [(5, load_dst_bc), (4, next_adst), (5, first_adst)] if first_layer else []))
            if first_layer:
                _, hi = window_bounds(sp, KSB - 1)
                sp.wait_ge(s_adw, (hi + KSB) * 16)
                sp.sem_inc(s_gate, 1)

        @block.gpsimd
        def _(pool):
            make_identity(nc, pool, ident, s_pool_setup)
            nc.gpsimd.iota(iota[:], pattern=[[1, WIN]], base=0, channel_multiplier=0,
                           allow_small_or_imprecise_dtypes=True).then_inc(s_pool_setup, 1)
            nc.gpsimd.iota(rowid[:], pattern=[[0, 1]], base=0, channel_multiplier=1,
                           allow_small_or_imprecise_dtypes=True).then_inc(s_pool_setup, 1)

            def gather(k, s):
                pool.wait_ge(s_idx[s], 16 * use(k, s, RING))
                ge(pool, s_msg, k - RING + 1)
                pool.sem_inc(s_go, 1)
                for j in range(J):
                    pool.indirect_dma_start(rows[s][:, j, :], None, table[:, :],
                                            bass.IndirectOffsetOnAxis(ap=idx[s][:, j:j + 1], axis=0))\
                        .then_inc(s_rows[s], 16)

            over_superblocks(pool, [(0, gather)])
            if not first_layer:
                pool.wait_ge(s_scan, KSB * SCAN)
                nc.gpsimd.partition_all_reduce(gmax[:], keep["gmax_part"][:], P, bass.bass_isa.ReduceOp.max)\
                    .then_inc(s_go, 1)
                pool.wait_ge(s_go, KSB + 1)

        @block.vector
        def _(dve):
            V = nc.vector
            V.memset(link[:], -BIG).then_inc(s_dve_setup, 1)
            V.memset(fwd_T[:], -BIG).then_inc(s_dve_setup, 1)
            V.memset(bwd_T[:], -BIG).then_inc(s_dve_setup, 1)
            V.memset(zero_row[:], 0.0).then_inc(s_dve_setup, 1)
            V.memset(att[0][:], 0.0).then_inc(s_setup, 1)
            dve.wait_ge(s_dve_setup, 4)
            dve.wait_ge(s_pool_setup, 4)
            scan, high = Chain(dve, s_scan), Chain(dve, s_max)
            hj = [P, H, J]
            flat = lambda t: t[:].rearrange("p h j -> p (h j)")

            def scores_and_scans(k, s):
                n, b, c = use(k, s, RING), s % 2, scan
                c.start(k * SCAN)
                dw = dwin[s]
                dve.wait_ge(s_dwin[s], 32 * n)
                if not first_layer:
                    ge(dve, s_fresh, FRESH * (k - 2) + 1)
                c.done(V.tensor_scalar(drel[s][:], dw[:, 0:J + 1], keep["base_f"][:, bass.ds(k, 1)], None, ALU.subtract))
                c.done(V.tensor_scalar(headmask[b][:], dw[:, 1:J + 1], dw[:, 0:1], -BIG, ALU.not_equal, ALU.mult))
                c.done(V.tensor_scalar(tailmask[b][:], dw[:, 1:J + 1], dw[:, J + 1:J + 2], -BIG, ALU.not_equal, ALU.mult))
                c.done(V.tensor_tensor(cut[b][:], dw[:, 1:J + 2], dw[:, 0:J + 1], ALU.not_equal))
                c.after()
                c.done(V.tensor_scalar(link[:, 0:HJ].rearrange("p (h j) -> p h j", h=H)[:, :, 1:J],
                                       bc(cut[b][:, 1:J], [P, H, J - 1], 1), -BIG, None, ALU.mult))
                ge(dve, s_ends, k)
                c.done(V.tensor_copy(edge_links[:, 0, :], headmask[b][:, J - 1:J].to_broadcast([P, H])))
                c.done(V.tensor_copy(edge_links[:, 1, :], tailmask[b][:, 0:1].to_broadcast([P, H])))
                ge(dve, s_z, 2 * k - 2)
                dve.wait_ge(s_rows[s], 16 * J * n)
                if first_layer:
                    dve.wait_ge(s_edge_score, k + 1)
                    c.done(V.tensor_tensor(score[b][:], rows[s][:, :, D:D + H].rearrange("p j h -> p h j"),
                                           edge_score[b][:].rearrange("p j h -> p h j"), ALU.add))
                else:
                    dve.wait_ge(s_att[s], att_landed(k, s))
                    up = rows[s][:, :, 2 * F1:2 * F1 + 2 * H1].rearrange("p j (d h) -> p d h j", d=2)
                    c.done(V.tensor_tensor(t0[:], up[:, 0], bc(att[s][:, :, 0], hj, 1), ALU.mult))
                    c.done(V.tensor_tensor(t1[:], up[:, 1], bc(att[s][:, :, 1], hj, 1), ALU.mult))
                    c.after()
                    c.done(V.tensor_tensor(t2[:], t0[:], t1[:], ALU.add))
                    c.after()
                    c.done(V.scalar_tensor_tensor(score[b][:], t2[:], 0.2, t2[:], ALU.mult, ALU.max))
                c.after()
                if not first_layer:
                    if isinstance(k, int) and k == 0:
                        c.done(V.tensor_scalar(t0[:, 0, :], dw[:, 1:J + 1], NO_NODE, -BIG, ALU.is_equal, ALU.mult))
                        c.after()
                        c.done(V.tensor_tensor(t1[:], score[b][:], bc(t0[:, 0, :], hj, 1), ALU.add))
                        c.after()
                        c.done(V.tensor_reduce(keep["gmax_part"][:], t1[:], AX_X, ALU.max))
                    else:
                        c.done(V.tensor_reduce(kmax[:], score[b][:], AX_X, ALU.max))
                        c.after()
                        c.done(V.tensor_tensor(keep["gmax_part"][:], keep["gmax_part"][:], kmax[:], ALU.max))
                        c.done(V.memset(t0[:, 0, 0:1], 0.0))
                c.done(V.tensor_tensor_scan(flat(fwd[b]), link[:, 0:HJ], flat(score[b]), -BIG, ALU.add, ALU.max))
                c.done(V.tensor_tensor_scan(flat(bwd[b])[:, ::-1], link[:, 1:HJ + 1][:, ::-1], flat(score[b])[:, ::-1],
                                            -BIG, ALU.add, ALU.max))
                assert c.n == SCAN, (layer, c.n)

            def scans_across(k, s):
                c = high
                c.start(k * MAX)
                c.done(V.tensor_copy(fwd_T[:, 0:1], fwd_T[:, P:P + 1]))
                scan.start(k * SCAN)
                scan.after(SCAN)
                c.done(V.tensor_tensor(local[:], fwd[s % 2][:], bwd[s % 2][:], ALU.max))
                c.after(1)
                dve.wait_ge(s_links_T, k + 1)
                V.tensor_tensor_scan(fwd_T[:, 1:P + 1], links_T[:, 0, :], ends_ps[:, 0, :], fwd_T[:, 0:1],
                                     ALU.add, ALU.max).then_inc(s_T, 1)
                V.tensor_tensor_scan(bwd_T[:, 0:P][:, ::-1], links_T[:, 1, :][:, ::-1], ends_ps[:, 1, :][:, ::-1],
                                     -BIG, ALU.add, ALU.max).then_inc(s_T, 1)

            def maxima(k, s):
                b, c = s % 2, high
                c.start(k * MAX)
                c.n = 2
                if first_layer:
                    dve.wait_ge(s_node_score, k + 1)
                    part = lambda q: node_parts[s][:, :, q * H:(q + 1) * H].rearrange("p j h -> p h j")
                    c.done(V.tensor_tensor(node_two[:], part(0), part(1), ALU.add))
                dve.wait_ge(s_back, k + 1)
                c.done(V.tensor_tensor(from_prev[:], bc(headmask[b][:], hj, 1), bc(back_ps[:, 0, :], hj, 2), ALU.add))
                c.done(V.tensor_tensor(from_next[:], bc(tailmask[b][:], hj, 1), bc(back_ps[:, 1, :], hj, 2), ALU.add))
                if first_layer:
                    c.after(3)
                    c.done(V.tensor_tensor(node_score[:], node_two[:], part(2), ALU.add))
                    c.after(5)
                    c.done(V.tensor_tensor(across[:], from_prev[:], from_next[:], ALU.max))
                    c.after(6)
                    c.done(V.tensor_tensor(both[:, 0], score[b][:], node_score[:], ALU.add))
                    c.done(V.tensor_tensor(old[:], from_prev[:, :, 0], node_score[:, :, 0], ALU.add))
                    c.after(7)
                    c.done(V.tensor_tensor(top[:], across[:], local[:], ALU.max))
                    c.after(9)
                    c.done(V.scalar_tensor_tensor(old_l[:], old[:], 0.01, old[:], ALU.mult, ALU.max))
                    c.after(10)
                    c.done(V.tensor_tensor(both[:, 1], top[:], node_score[:], ALU.add))
                    c.after()
                    c.done(V.scalar_tensor_tensor(both_l[:], both[:], 0.01, both[:], ALU.mult, ALU.max))
                    c.after()
                    score_l, top_l, old_v = both_l[:, 0], both_l[:, 1], old_l[:]
                else:
                    c.after()
                    c.done(V.tensor_tensor(across[:], from_prev[:], from_next[:], ALU.max))
                    c.after()
                    c.done(V.tensor_tensor(top[:], across[:], local[:], ALU.max))
                    c.after()
                    score_l, top_l, old_v = score[b][:], top[:], from_prev[:, :, 0]
                assert c.n == MAX, (layer, c.n)
                ge(dve, s_exp, 2 * k)
                V.tensor_tensor(z[:], score_l, top_l, ALU.subtract).then_inc(s_z, 1)
                V.tensor_tensor(z_old[:], old_v, top_l[:, :, 0], ALU.subtract).then_inc(s_z, 1)

            def products(k, s):
                b = s % 2
                m = msg[b]
                dve.wait_ge(s_exp, 2 * k + 2)
                heads = m[:, :, 0:D].rearrange("p j (h f) -> p j h f", h=H)
                if first_layer:
                    V.tensor_tensor(heads, rows[s][:, :, 0:D].rearrange("p j (h f) -> p j h f", h=H),
                                    bc(m[:, :, D:D + H], [P, J, H, F0], 3), ALU.mult).then_inc(s_msg, 1)
                else:
                    prod = Chain(dve, s_prod)
                    prod.start(k)
                    dve.wait_ge(s_mix, 2 * J * k + 2 * J)
                    prod.done(V.tensor_tensor(mix[:], fwd_msg[b][:], rev_msg[b][:], ALU.add))
                    prod.after()
                    V.tensor_tensor(heads, bc(mix[:], [P, J, H, F1], 2), bc(m[:, :, D:D + H], [P, J, H, F1], 3),
                                    ALU.mult).then_inc(s_msg, 1)

            def carry_on(k, s):
                if isinstance(k, int) and k == 0:
                    V.memset(carry[:, 0:D], 0.0).then_inc(s_fresh, 1)
                    V.memset(carry[:, D:W], 0.0).then_inc(s_fresh, 1)
                    return
                dve.wait_ge(s_carry, k)
                V.tensor_tensor(carry[:, 0:D].rearrange("p (h f) -> p h f", h=H),
                                carry_ps[:, 0:D].rearrange("p (h f) -> p h f", h=H),
                                bc(fade[0:1, :], [1, H, D // H], 2), ALU.mult).then_inc(s_fresh, 1)
                V.tensor_tensor(carry[:, D:W].rearrange("p (g h) -> p g h", h=H),
                                carry_ps[:, D:W].rearrange("p (g h) -> p g h", h=H),
                                bc(fade[0:1, :], [1, 8 // H, H], 1), ALU.mult).then_inc(s_fresh, 1)

            def onehots(s, ready):
                b = s % 2
                V.tensor_tensor(onehot[b][:], bc(iota[:], [P, J, WIN], 1), bc(drel[s][:, 1:J + 1], [P, J, WIN], 2),
                                ALU.is_equal).then_inc(ready, 1)
                V.tensor_scalar(onehot_carry[b][:], iota[0:1, :], drel[s][0:1, 0:1], None, ALU.is_equal)\
                    .then_inc(ready, 1)

            def first_onehots(k, s):
                onehots(s, s_hot)
                V.tensor_scalar(pick_last[s % 2][:], rowid[0:WIN, :], keep["last_rel"][0:WIN, bass.ds(k, 1)], None,
                                ALU.is_equal).then_inc(s_hot, 1)

            def next_onehots(k, s):
                lo, hi = window_bounds(dve, k)
                with dve.Fori(lo, hi) as w:
                    dve.wait_ge(s_mm, w + 1)
                    V.tensor_scalar(drel[s][:], drel[s][:], -float(WIN), None, ALU.add).then_inc(s_next_hot, 1)
                    dve.wait_ge(s_next_hot, 3 * w + 2)
                    onehots(s, s_next_hot)
                    dve.wait_ge(s_next_hot, 3 * w + 4)

            def segment_maximum(k, s):
                V.tensor_tensor(msg[s % 2][:, :, D + H:W].rearrange("p j h -> p h j"), top[:],
                                bc(cut[s % 2][:, 1:J + 1], hj, 1), ALU.mult).then_inc(s_fresh, 1)

            dve.sem_inc(s_next_hot, 1)
            over_superblocks(dve, [(1, maxima)] + ([] if first_layer else [(1, segment_maximum)]) + [
                (3, scores_and_scans), (2, scans_across), (1, first_onehots), (1, products), (0, next_onehots),
                (1, carry_on)])

        @block.scalar
        def _(act):
            def node_onehots(i, b):
                act.wait_ge(s_act, i * 3 + 1)
                nc.scalar.activation(dist[:], dst_bc[b][:], ACT.Abs, bias=minus_node[:, 0:1]).then_inc(s_act, 1)
                act.wait_ge(s_act, i * 3 + 2)
                nc.scalar.activation(node_hot[:], dist[:], ACT.Relu, bias=1.0, scale=-1.0).then_inc(s_node_hot, 1)
                act.wait_ge(s_node_hot, i + 1)
                act.sem_inc(s_act, 1)

            def first_node_onehots(k, s):
                lo, _ = window_bounds(act, k)
                i, b = act.snap(lo + k), s % 2
                nc.scalar.copy(minus_node[:], keep["minus_node"][0:WIN, bass.ds(k, 1)]).then_inc(s_act, 1)
                act.wait_ge(s_dstbc[b], 16 * use(k, b, 2))
                node_onehots(i, b)

            def next_node_onehots(k, s):
                lo, hi = window_bounds(act, k)
                with act.Fori(lo, hi) as w:
                    i = act.snap(w + (k + 1))
                    act.wait_ge(s_spread, w + 1)
                    nc.scalar.activation(minus_node[:], minus_node[:], ACT.Copy, bias=-float(WIN)).then_inc(s_act, 1)
                    node_onehots(i, s % 2)
                act.sem_inc(s_dstbc_used, 1)

            def copy_att(k, s):
                act.wait_ge(s_attp, k + 1)
                ge(act, s_ae, k)
                nc.scalar.copy(att_T[:], att_ps).then_inc(s_attT, 1)

            def copy_node_parts(k, s):
                ge(act, s_z, 2 * (k - RING) + 2)
                act.wait_ge(s_ad, k + 1)
                nc.scalar.copy(node_parts[s][:], ad_ps).then_inc(s_node_score, 1)

            def copy_edge_score(k, s):
                ge(act, s_scan, (k - 1) * SCAN)
                act.wait_ge(s_ae, k + 1)
                nc.scalar.copy(edge_score[s % 2][:], ae_ps).then_inc(s_edge_score, 1)

            def exps(k, s):
                act.wait_ge(s_z, 2 * k + 2)
                ge(act, s_fresh, FRESH * k)
                nc.scalar.activation(msg[s % 2][:, :, D:D + H].rearrange("p j h -> p h j"), z[:], ACT.Exp)\
                    .then_inc(s_exp, 1)
                nc.scalar.activation(fade[:], z_old[:], ACT.Exp).then_inc(s_exp, 1)

            def links(k, s):
                act.wait_ge(s_ends, k + 1)
                ge(act, s_T, 2 * k)
                nc.scalar.copy(links_T[:], ends_ps[:, 2:4, :]).then_inc(s_links_T, 1)

            def directed(k, s):
                b = s % 2
                act.wait_ge(s_rows[s], 16 * J * use(k, s, RING))
                act.wait_ge(s_att[s], att_landed(k, s))
                ge(act, s_msg, k - 1)
                for j in range(J):
                    nc.scalar.activation(fwd_msg[b][:, j, :], rows[s][:, j, 0:F1], ACT.Copy,
                                         scale=att[s][:, j, 0:1]).then_inc(s_mix, 1)
                    nc.scalar.activation(rev_msg[b][:, j, :], rows[s][:, j, F1:2 * F1], ACT.Copy,
                                         scale=att[s][:, j, 1:2]).then_inc(s_mix, 1)
                act.wait_ge(s_mix, 2 * J * k + 2 * J)
                act.sem_inc(s_att_used, 1)

            def evacuate(k, s):
                base = act.value_load(keep["base_i"][0:1, bass.ds(k, 1)], min_val=0, max_val=N - 1)
                lo, hi = window_bounds(act, k)
                with act.Fori(lo, hi) as w:
                    row = window_row(act, base, w, lo)
                    act.wait_ge(s_mm, w + 1)
                    act.wait_ge(s_stored, 16 * w + 16)
                    ge(act, s_carry, k)
                    nc.scalar.copy(out_rows[:], sums_ps).then_inc(s_out, 1)
                    act.wait_ge(s_out, w + 2)
                    act.dma_start(acc[bass.ds(row, WIN), :], out_rows[:]).then_inc(s_stored, 16)

            act.sem_inc(s_stored, 16)
            over_superblocks(act, [(1, exps), (2, links), (4, first_node_onehots) if first_layer else (2, directed),
                                   (0, evacuate)] + (
                [(4, copy_att), (4, next_node_onehots), (4, copy_node_parts), (4, copy_edge_score)]
                if first_layer else []))
            _, hi = window_bounds(act, KSB - 1)
            act.wait_ge(s_stored, 16 * hi + 16)
            act.sem_inc(s_gate, 1)

        @block.tensor
        def _(pe):
            pe.wait_ge(s_pool_setup, 4)
            pe.wait_ge(s_dve_setup, 4)
            bounds = {}

            def sum_bounds(k, s):
                bounds["sum"] = window_bounds(pe, k)

            def turn_att(k, s):
                pe.wait_ge(s_att[s], att_landed(k, s))
                ge(pe, s_attT, k)
                for q in range(J // 2):
                    last = nc.tensor.transpose(att_ps[:, q, :], att[s][:, 2 * q:2 * q + 2, :].rearrange("p j c -> p (j c)"),
                                               ident[:])
                last.then_inc(s_attp, 1)

            def spread(k, s):
                flat = ad_ps.rearrange("p j h -> p (j h)")
                lo, hi = bounds["spread"]
                ge(pe, s_node_score, k)
                nc.tensor.matmul(flat, zero_row[:, 0:P], zero_row[:, 0:3 * HJ], start=True, stop=False,
                                 skip_group_check=True)
                with pe.Fori(lo, hi) as w:
                    pe.wait_ge(s_node_hot, w + (k + 1))
                    pe.wait_ge(s_adw, (w + (k + 1)) * 16)
                    hot = node_hot[:].rearrange("p (e j) -> p j e", j=J)
                    for j in range(J):
                        last = nc.tensor.matmul(ad_ps[:, j, :], hot[:, j, :], adst_win[:], start=False, stop=False,
                                                skip_group_check=True)
                    last.then_inc(s_spread, 1)
                nc.tensor.matmul(flat, zero_row[:, 0:P], zero_row[:, 0:3 * HJ], start=False, stop=True,
                                 skip_group_check=True).then_inc(s_ad, 1)

            def edge_scores(k, s):
                pe.wait_ge(s_attT, k + 1)
                ge(pe, s_edge_score, k)
                for q in range(J // 2):
                    last = nc.tensor.matmul(ae_ps[:, 2 * q:2 * q + 2, :].rearrange("p j h -> p (j h)"),
                                            att_T[:, q, :], edge_w[:], start=True, stop=True)
                last.then_inc(s_ae, 1)
                pe.sem_inc(s_att_used, 1)

            def turn_ends(k, s):
                pe.wait_ge(s_scan, (k + 1) * SCAN)
                ge(pe, s_T, 2 * k)
                ge(pe, s_links_T, k)
                nc.tensor.transpose(ends_ps[:, 0, :], fwd[s % 2][:, :, J - 1], ident[:])
                nc.tensor.transpose(ends_ps[:, 1, :], bwd[s % 2][:, :, 0], ident[:])
                nc.tensor.transpose(ends_ps[:, 2, :], edge_links[:, 0, :], ident[:])
                nc.tensor.transpose(ends_ps[:, 3, :], edge_links[:, 1, :], ident[:]).then_inc(s_ends, 1)

            def turn_back(k, s):
                pe.wait_ge(s_T, 2 * k + 2)
                ge(pe, s_z, 2 * k)
                pe.sem_inc(s_gate, 1)
                nc.tensor.transpose(back_ps[:, 0, :], fwd_T[:, 0:P], ident[0:H, 0:H])
                nc.tensor.transpose(back_ps[:, 1, :], bwd_T[:, 1:P + 1], ident[0:H, 0:H]).then_inc(s_back, 1)

            def sum_windows(k, s):
                b = s % 2
                lo, hi = bounds["sum"]
                with pe.Fori(lo, hi) as w:
                    pe.wait_ge(s_msg, k + 1)
                    pe.wait_ge(s_hot, 3 * k + 3)
                    pe.wait_ge(s_next_hot, 3 * w + 1)
                    pe.wait_ge(s_out, w + 1)
                    for j in range(J):
                        nc.tensor.matmul(sums_ps, onehot[b][:, j, :], msg[b][:, j, :], start=(j == 0), stop=False)
                    pe.wait_ge(s_fresh, FRESH * k + FRESH)
                    pe.sem_inc(s_gate, 1)
                    nc.tensor.matmul(sums_ps, onehot_carry[b][:], carry[:], start=False, stop=True).then_inc(s_mm, 1)
            def spread_bounds(k, s):
                bounds["spread"] = window_bounds(pe, k)

            def pick(k, s):
                pe.wait_ge(s_out, bounds["sum"][1] + 1)
                pe.sem_inc(s_gate, 1)
                nc.tensor.matmul(carry_ps, pick_last[s % 2][:], out_rows[:], start=True, stop=True).then_inc(s_carry, 1)

            pe.sem_inc(s_out, 1)
            over_superblocks(pe, [(0, sum_bounds), (2, turn_ends), (0, sum_windows)] + (
                [(4, turn_att), (4, spread_bounds), (0, pick), (2, turn_back), (4, spread), (4, edge_scores)]
                if first_layer else [(0, pick), (2, turn_back)]))


def final_stage(nc, x1, acc, gmax, out):
    with ExitStack() as ctx:
        def sb(name, shape, dt=F32):
            return ctx.enter_context(nc.sbuf_tensor("f_" + name, shape, dt))

        def sem(name):
            return ctx.enter_context(nc.semaphore("f_" + name))

        xs = sb("x", [P, T, D])
        sums = sb("sums", [P, T, W])
        gap = sb("gap", [P, T, H1])
        gap_exp = sb("gap_exp", [P, T, H1])
        den = sb("den", [P, T, H1])
        rden = sb("rden", [P, T, H1])
        s_x = [sem(f"x_in{n}") for n in range(4)]
        s_sums = [sem(f"sums_in{n}") for n in range(4)]
        s_gap = sem("gap_ready")
        s_exp = sem("exp_ready")
        s_dve = sem("steps")
        s_y = sem("y_ready")
        s_st = sem("stored")
        block = ctx.enter_context(nc.Block())

        @block.sync
        def _(sp):
            for n in range(4):
                move_chunk(sp, n, sums, acc, s_sums[n])
                move_chunk(sp, n, xs, x1, s_x[n])
            for n in range(4):
                sp.wait_ge(s_y, n + 1)
                move_chunk(sp, n, xs, out, s_st, to_dram=True)
            sp.wait_ge(s_st, 80)

        @block.vector
        def _(dve):
            c = Chain(dve, s_dve)

            def gaps(n):
                a, b = CHUNKS[n]
                dve.wait_ge(s_sums[n], 32 if n == 3 else 16)
                nc.vector.tensor_tensor(gap[:, a:b], bc(gmax[:], [P, b - a, H1], 1), sums[:, a:b, D + H1:W],
                                        ALU.subtract).then_inc(s_gap, 1)

            gaps(0)
            for n, (a, b) in enumerate(CHUNKS):
                dve.wait_ge(s_exp, n + 1)
                c.done(nc.vector.scalar_tensor_tensor(den[:, a:b], gap_exp[:, a:b], 1e-10, sums[:, a:b, D:D + H1],
                                                      ALU.mult, ALU.add))
                c.after()
                c.done(nc.vector.reciprocal(rden[:, a:b], den[:, a:b]))
                c.after()
                heads = sums[:, a:b, 0:D].rearrange("p t (h f) -> p t h f", h=H1)
                c.done(nc.vector.tensor_tensor(heads, heads, bc(rden[:, a:b], [P, b - a, H1, F1], 3), ALU.mult))
                dve.wait_ge(s_x[n], 32 if n == 3 else 16)
                c.after()
                nc.vector.tensor_tensor(xs[:, a:b], sums[:, a:b, 0:D], xs[:, a:b], ALU.add).then_inc(s_y, 1)
                if n < 3:
                    gaps(n + 1)

        @block.scalar
        def _(act):
            for n, (a, b) in enumerate(CHUNKS):
                act.wait_ge(s_gap, n + 1)
                nc.scalar.activation(gap_exp[:, a:b], gap[:, a:b], ACT.Exp).then_inc(s_exp, 1)


def gnn_kernel(nc, x, src, dst, edge_attr_2, edge_attr_64, W_w, We_w, a_src, a_dst, a_edge, W_forward, W_reverse,
               attn_forward, out):
    table0 = nc.dram_tensor("table0", [N, W], F32).ap()
    table1 = nc.dram_tensor("table1", [N, W1], F32).ap()
    adst = nc.dram_tensor("adst", [NROWS, 3 * H0], BF16).ap()
    acc0 = nc.dram_tensor("acc0", [NROWS, W], F32).ap()
    acc1 = nc.dram_tensor("acc1", [NROWS, W], F32).ap()
    x1 = nc.dram_tensor("x1", [N, D], F32).ap()
    dst_f = nc.dram_tensor("dst_f", [KSB * SB + J + 2], F32).ap()
    src_pad = nc.dram_tensor("src_pad", [KSB * SB], I32).ap()
    with ExitStack() as ctx:
        def sb(name, shape, dt=F32):
            return ctx.enter_context(nc.sbuf_tensor(name, shape, dt))

        keep = {
            "base_i": sb("base_i", [1, KSB], I32), "win_i": sb("win_i", [1, KSB + 1], I32),
            "base_f": sb("base_f", [P, KSB]), "last_rel": sb("last_rel_all", [P, KSB]),
            "minus_node": sb("minus_node_all", [P, KSB]), "edge_w": sb("edge_w", [P, 2 * H0]),
            "gmax_part": sb("gmax_part", [P, H1]),
        }
        gmax = sb("gmax", [P, H1])
        rings = [[ctx.enter_context(nc.semaphore(f"{name}_in{s}")) for s in range(RING)]
                 for name in ("idx", "dwin", "att", "rows")]
        edge_tables(nc, src, dst, dst_f, src_pad, adst, keep)
        node_stage(nc, 0, x, None, None, table0, adst,
                   {"W": W_w, "We": We_w, "a_src": a_src, "a_dst": a_dst, "a_edge": a_edge}, keep, clear=(acc0, acc1))
        edge_stage(nc, 0, table0, dst_f, src_pad, edge_attr_64, adst, acc0, keep, gmax, rings)
        node_stage(nc, 1, x, acc0, x1, table1, None, {"Wf": W_forward, "Wr": W_reverse, "attn": attn_forward}, keep)
        edge_stage(nc, 1, table1, dst_f, src_pad, edge_attr_2, None, acc1, keep, gmax, rings)
        final_stage(nc, x1, acc1, gmax, out)


_INS = ['x', 'src', 'dst', 'edge_attr_2', 'edge_attr_64', 'L0_gnn_W_w', 'L0_gnn_We_w', 'L0_gnn_a_src', 'L0_gnn_a_dst',
        'L0_gnn_a_edge', 'L1_gnn_W_forward', 'L1_gnn_W_reverse', 'L1_gnn_attn_forward']
_OUTS = [((6250, 256), 'float32')]


def kernel(**inputs):
    import numpy as _np
    import concourse.bacc as _bacc
    from concourse import mybir as _mybir
    from concourse.bass_utils import run_bass_kernel_spmd as _run

    nc = _bacc.Bacc("TRN2", target_bir_lowering=False, num_devices=1)
    arrays, args = {}, []
    for name in _INS:
        a = _np.ascontiguousarray(inputs[name])
        arrays[f"in_{name}_dram"] = a
        args.append(nc.dram_tensor(f"in_{name}_dram", a.shape, _mybir.dt.from_np(a.dtype), kind="ExternalInput").ap())
    for i, (shape, dtype) in enumerate(_OUTS):
        dt = _mybir.dt.from_np(_np.dtype(dtype))
        args.append(nc.dram_tensor(f"out_{i}_dram", shape, dt, kind="ExternalOutput").ap())
    gnn_kernel(nc, *args)
    r = _run(nc, [arrays], core_ids=[0])
    got = tuple(r.results[0][f"out_{i}_dram"] for i in range(len(_OUTS)))
    return got[0]
```
